# Optimizing a Trainium2 kernel written in Bass

```python
import numpy as np
import jax
import jax.numpy as jnp

def _softmax(x, axis=-1):
    return jax.nn.softmax(x, axis=axis)

def _gelu(x):
    return jax.nn.gelu(x, approximate=True)

def _silu(x):
    return jax.nn.silu(x)

def _sigmoid(x):
    return jax.nn.sigmoid(x)

def _layernorm(x, axis=-1, eps=1e-05):
    m = jnp.mean(x, axis=axis, keepdims=True)
    v = jnp.var(x, axis=axis, keepdims=True)
    return (x - m) / jnp.sqrt(v + eps)

def _scatter_add(tgt, idx, src, axis=0):
    return tgt.at[idx].add(src)

def _segment_sum(src, seg, n):
    return jax.ops.segment_sum(src, seg, n)
kernel_name = 'mk_adaln_attn_ffn_d1_seqx_r8_cedd83'

def setup_inputs(seed: int=0):
    np.random.seed(seed)
    _w = jnp.asarray

    def _rec_inputs():
        import jax
        import jax.numpy as jnp
        _rk = jax.random.key(seed)
        x = -1.528e-05 + 0.9999 * jax.random.normal(jax.random.fold_in(_rk, 1), (32, 128, 128), jnp.float32)
        _lenS = 128 - jax.random.randint(jax.random.fold_in(_rk, 7), (32,), 0, max(1, 128 // 4) + 1, jnp.int32)
        _lenS2 = 128 - jax.random.randint(jax.random.fold_in(_rk, 8), (32,), 0, max(1, 128 // 4) + 1, jnp.int32)
        cond_1024 = -0.00608245 + 1.00131 * jax.random.normal(jax.random.fold_in(_rk, 11), (32, 128), jnp.float32)
        return (x, cond_1024)
    x, cond_1024 = _rec_inputs()

    def _L0_cond_setup():
        import jax, jax.numpy as jnp
        import numpy as np
        LATENT = 128
        key = jax.random.key(seed)
        k1, k2, k3, k4 = jax.random.split(key, 4)
        B, T, D = (64, 64, LATENT)
        h_t = jax.random.normal(k1, (B, D), dtype=jnp.float32)
        z = jax.random.normal(k2, (B, T, D), dtype=jnp.float32)
        bound = 1.0 / np.sqrt(2 * D)
        W = jax.random.uniform(k3, (D, 2 * D), minval=-bound, maxval=bound, dtype=jnp.float32)
        b = jax.random.uniform(k4, (D,), minval=-bound, maxval=bound, dtype=jnp.float32)
        alpha = jnp.full((D,), 0.1, dtype=jnp.float32)
        return {'h_t': h_t, 'z': z, 'W': W, 'b': b, 'alpha': alpha}
    _L0_cond_all = _L0_cond_setup()
    _L0_cond_in = {k: v for k, v in _L0_cond_all.items() if k in ('W', 'b', 'alpha')}
    del _L0_cond_all

    def _L0_attn_setup():
        import jax, jax.numpy as jnp
        import numpy as np
        NUM_HEADS = 16
        MAX_REL = 128

        def _rel_embeds(table, q_len, k_len):
            dist = jnp.arange(q_len)[:, None] - jnp.arange(k_len)[None, :]
            idx = jnp.clip(dist, -MAX_REL, MAX_REL) + MAX_REL
            return table[idx]
        key = jax.random.key(seed)
        ks = jax.random.split(key, 11)
        B, T, E = (4, 128, 128)
        D = E // NUM_HEADS
        P = 2 * MAX_REL + 1
        s = 0.02
        return {'hidden_states': jax.random.normal(ks[0], (B, T, E), jnp.float32), 'Wq': jax.random.normal(ks[1], (E, E), jnp.float32) * s, 'bq': jax.random.normal(ks[2], (E,), jnp.float32) * s, 'Wk': jax.random.normal(ks[3], (E, E), jnp.float32) * s, 'bk': jax.random.normal(ks[4], (E,), jnp.float32) * s, 'Wv': jax.random.normal(ks[5], (E, E), jnp.float32) * s, 'bv': jax.random.normal(ks[6], (E,), jnp.float32) * s, 'Wo': jax.random.normal(ks[7], (E, E), jnp.float32) * s, 'bo': jax.random.normal(ks[8], (E,), jnp.float32) * s, 'rel_k_emb': jax.random.normal(ks[9], (P, D), jnp.float32) * s, 'rel_v_emb': jax.random.normal(ks[10], (P, D), jnp.float32) * s}
    _L0_attn_all = _L0_attn_setup()
    _L0_attn_in = {k: v for k, v in _L0_attn_all.items() if k in ('Wq', 'bq', 'Wk', 'bk', 'Wv', 'bv', 'Wo', 'bo', 'rel_k_emb', 'rel_v_emb')}
    del _L0_attn_all

    def _L0_cond2_setup():
        import jax, jax.numpy as jnp
        import numpy as np
        N, T, D, H = (128, 64, 128, 128)
        key = jax.random.key(seed)
        k1, k2, k3, k4 = jax.random.split(key, 4)
        x = jax.random.normal(k1, (N, T, D), dtype=jnp.float32)
        h0 = jax.random.normal(k2, (N, H), dtype=jnp.float32)
        Wx = jax.random.normal(k3, (D, H), dtype=jnp.float32) / np.sqrt(D)
        Wh = jax.random.normal(k4, (H, H), dtype=jnp.float32) / np.sqrt(H)
        b = jnp.zeros((H,), dtype=jnp.float32)
        return {'x': x, 'h0': h0, 'Wx': Wx, 'Wh': Wh, 'b': b}
    _L0_cond2_all = _L0_cond2_setup()
    _L0_cond2_in = {k: v for k, v in _L0_cond2_all.items() if k in ('Wx', 'Wh', 'b')}
    del _L0_cond2_all

    def _L0_ffn_setup():
        import jax, jax.numpy as jnp
        import numpy as np
        TOP_K = 2
        key = jax.random.key(seed)
        ks = jax.random.split(key, 5)
        B, N, C, FF, E = (2, 256, 128, 512, 8)
        x = jax.random.normal(ks[0], (B, N, C), dtype=jnp.float32)
        router_w = jax.random.normal(ks[1], (E, C), dtype=jnp.float32) * 0.02
        lim1 = np.sqrt(6.0 / (FF + C))
        expert_w1 = jax.random.uniform(ks[2], (E, FF, C), dtype=jnp.float32, minval=-lim1, maxval=lim1)
        expert_b1 = jnp.zeros((E, FF), dtype=jnp.float32)
        expert_w2 = jax.random.uniform(ks[3], (E, C, FF), dtype=jnp.float32, minval=-lim1, maxval=lim1)
        expert_b2 = jnp.zeros((E, C), dtype=jnp.float32)
        return {'x': x, 'router_w': router_w, 'expert_w1': expert_w1, 'expert_b1': expert_b1, 'expert_w2': expert_w2, 'expert_b2': expert_b2}
    _L0_ffn_all = _L0_ffn_setup()
    _L0_ffn_in = {k: v for k, v in _L0_ffn_all.items() if k in ('router_w', 'expert_w1', 'expert_b1', 'expert_w2', 'expert_b2')}
    del _L0_ffn_all
    return {'x': x, 'cond_1024': cond_1024, 'L0_cond_W': _L0_cond_in['W'], 'L0_cond_b': _L0_cond_in['b'], 'L0_cond_alpha': _L0_cond_in['alpha'], 'L0_attn_Wq': _L0_attn_in['Wq'], 'L0_attn_bq': _L0_attn_in['bq'], 'L0_attn_Wk': _L0_attn_in['Wk'], 'L0_attn_bk': _L0_attn_in['bk'], 'L0_attn_Wv': _L0_attn_in['Wv'], 'L0_attn_bv': _L0_attn_in['bv'], 'L0_attn_Wo': _L0_attn_in['Wo'], 'L0_attn_bo': _L0_attn_in['bo'], 'L0_attn_rel_k_emb': _L0_attn_in['rel_k_emb'], 'L0_attn_rel_v_emb': _L0_attn_in['rel_v_emb'], 'L0_cond2_Wx': _L0_cond2_in['Wx'], 'L0_cond2_Wh': _L0_cond2_in['Wh'], 'L0_cond2_b': _L0_cond2_in['b'], 'L0_ffn_router_w': _L0_ffn_in['router_w'], 'L0_ffn_expert_w1': _L0_ffn_in['expert_w1'], 'L0_ffn_expert_b1': _L0_ffn_in['expert_b1'], 'L0_ffn_expert_w2': _L0_ffn_in['expert_w2'], 'L0_ffn_expert_b2': _L0_ffn_in['expert_b2']}

def reference(x, cond_1024, L0_cond_W, L0_cond_b, L0_cond_alpha, L0_attn_Wq, L0_attn_bq, L0_attn_Wk, L0_attn_bk, L0_attn_Wv, L0_attn_bv, L0_attn_Wo, L0_attn_bo, L0_attn_rel_k_emb, L0_attn_rel_v_emb, L0_cond2_Wx, L0_cond2_Wh, L0_cond2_b, L0_ffn_router_w, L0_ffn_expert_w1, L0_ffn_expert_b1, L0_ffn_expert_w2, L0_ffn_expert_b2):
    import jax
    import jax.numpy as jnp

    def _L0_cond_ref(h_t, z, W, b, alpha):
        import jax, jax.numpy as jnp
        import numpy as np
        LATENT = 128
        D = h_t.shape[-1]
        Wh = W[:, :D]
        Wz = W[:, D:]
        leak = 1.0 - alpha

        def step(h, z_t):
            gate = jax.nn.sigmoid(h @ Wh.T + z_t @ Wz.T + b)
            h_new = jnp.tanh(h * leak + gate * z_t)
            return (h_new, h_new)
        _, hs = jax.lax.scan(step, h_t, jnp.swapaxes(z, 0, 1))
        return jnp.swapaxes(hs, 0, 1)

    def _L0_attn_ref(hidden_states, Wq, bq, Wk, bk, Wv, bv, Wo, bo, rel_k_emb, rel_v_emb):
        import jax, jax.numpy as jnp
        import numpy as np
        NUM_HEADS = 16
        MAX_REL = 128

        def _rel_embeds(table, q_len, k_len):
            dist = jnp.arange(q_len)[:, None] - jnp.arange(k_len)[None, :]
            idx = jnp.clip(dist, -MAX_REL, MAX_REL) + MAX_REL
            return table[idx]
        B, T, E = hidden_states.shape
        H = NUM_HEADS
        D = E // H
        scaling = jnp.sqrt(jnp.asarray(D, hidden_states.dtype))
        q = hidden_states @ Wq.T + bq
        k = hidden_states @ Wk.T + bk
        v = hidden_states @ Wv.T + bv
        qh = q.reshape(B, T, H, D).transpose(0, 2, 1, 3)
        kh = k.reshape(B, T, H, D).transpose(0, 2, 1, 3)
        vh = v.reshape(B, T, H, D).transpose(0, 2, 1, 3)
        score1 = jnp.einsum('bhqd,bhkd->bhqk', qh, kh)
        rel_k = _rel_embeds(rel_k_emb, T, T)
        s2 = jnp.einsum('bhqd,qkd->qbhk', qh, rel_k)
        s2 = s2.reshape(T, H, B, T).transpose(2, 1, 0, 3)
        scores = (score1 + s2) / scaling
        attn = jax.nn.softmax(scores, axis=-1)
        w1 = jnp.einsum('bhqk,bhkd->bhqd', attn, vh)
        rel_v = _rel_embeds(rel_v_emb, T, T)
        se = attn.reshape(B * H, T, T).transpose(1, 0, 2)
        w2 = jnp.einsum('qnk,qkd->qnd', se, rel_v)
        w2 = w2.reshape(T, H, B, D).transpose(2, 1, 0, 3)
        out = (w1 + w2).transpose(0, 2, 1, 3).reshape(B, T, E)
        return out @ Wo.T + bo

    def _L0_cond2_ref(x, h0, Wx, Wh, b):
        import jax, jax.numpy as jnp
        import numpy as np
        N, T, D, H = (128, 64, 128, 128)
        xp = jnp.einsum('ntd,dh->nth', x, Wx) + b

        def step(prev_h, xp_t):
            next_h = jnp.tanh(xp_t + prev_h @ Wh)
            return (next_h, next_h)
        _, h = jax.lax.scan(step, h0, jnp.swapaxes(xp, 0, 1))
        return jnp.swapaxes(h, 0, 1)

    def _L0_ffn_ref(x, router_w, expert_w1, expert_b1, expert_w2, expert_b2):
        import jax, jax.numpy as jnp
        import numpy as np
        TOP_K = 2
        router_logits = jnp.einsum('bnc,ec->bne', x, router_w)
        router_probs = jax.nn.softmax(router_logits, axis=-1)
        expert_weights, expert_idx = jax.lax.top_k(router_probs, TOP_K)
        expert_weights = expert_weights / (expert_weights.sum(axis=-1, keepdims=True) + 1e-09)
        h = jnp.einsum('bnc,efc->bnef', x, expert_w1) + expert_b1
        h = jax.nn.gelu(h, approximate=False)
        out_all = jnp.einsum('bnef,ecf->bnec', h, expert_w2) + expert_b2
        out_k = jnp.take_along_axis(out_all, expert_idx[..., None], axis=2)
        return (out_k * expert_weights[..., None]).sum(axis=2)
    x = x + _L0_attn_ref(_L0_cond_ref(cond_1024, x, L0_cond_W, L0_cond_b, L0_cond_alpha), L0_attn_Wq, L0_attn_bq, L0_attn_Wk, L0_attn_bk, L0_attn_Wv, L0_attn_bv, L0_attn_Wo, L0_attn_bo, L0_attn_rel_k_emb, L0_attn_rel_v_emb)
    x = x + _L0_ffn_ref(_L0_cond2_ref(x, cond_1024, L0_cond2_Wx, L0_cond2_Wh, L0_cond2_b), L0_ffn_router_w, L0_ffn_expert_w1, L0_ffn_expert_b1, L0_ffn_expert_w2, L0_ffn_expert_b2)
    return x

_drawn_inputs = setup_inputs


def setup_inputs(seed=0):
    import zlib

    import numpy as np

    out = dict(_drawn_inputs(seed))
    spreads = {'L0_cond_alpha': (0.10000000149011612, 0.6),
     'L0_cond2_b': (0.0, 0.1),
     'L0_ffn_expert_b1': (0.0, 0.1),
     'L0_ffn_expert_b2': (0.0, 0.1)}
    factors = {'L0_cond_W': 5.983,
     'L0_cond_b': 22.788,
     'L0_attn_Wq': 8.0,
     'L0_attn_bq': 21.374,
     'L0_attn_Wk': 8.0,
     'L0_attn_bk': 64.0,
     'L0_attn_Wv': 3.492,
     'L0_attn_bv': 3.392,
     'L0_attn_Wo': 2.963,
     'L0_attn_rel_k_emb': 24.8,
     'L0_attn_rel_v_emb': 8.0}
    for name, (base, spread) in spreads.items():
        noise = np.random.default_rng([zlib.crc32(name.encode()), seed]).standard_normal(out[name].shape)
        drawn = base * np.exp(spread * noise) if base else spread * noise
        out[name] = jnp.asarray(drawn.astype(out[name].dtype))
    for name, factor in factors.items():
        out[name] = (out[name] * factor).astype(out[name].dtype)
    return out
```

```python
from contextlib import ExitStack

import concourse.bass as bass
from concourse import mybir

F32 = mybir.dt.float32
U32 = mybir.dt.uint32
ALU = mybir.AluOpType
ACT = mybir.ActivationFunctionType
AX = mybir.AxisListType

P = 128
B = 32
T = 128
D = 128
H = 16
DH = D // H
QUAD = 4
NHG = H // QUAD
BANK = 512
E = 8
FF = 512
FC = FF // P
TC = BANK // B
NCH = T // TC
JT = BANK // P
GB = 8
NG = B // GB
REL = 2 * T - 1
QS = 16
SEG = QS + T - 1


def build(nc, a):
    with ExitStack() as ctx:
        def sb(name, shape, dt=F32):
            return ctx.enter_context(nc.sbuf_tensor(name, shape, dt))

        def sem(name):
            return ctx.enter_context(nc.semaphore(name))

        s2_dram = nc.dram_tensor("s2_scratch", (H * B, T, T), F32).ap()
        w2_dram = nc.dram_tensor("w2_scratch", (T * DH, H * B), F32).ap()

        ident = sb("ident", [P, P])
        hmask = sb("hmask", [P, QUAD])
        xT = sb("xT", [P, T, B])
        gate = sb("gate", [P, B])
        upd = sb("upd", [P, B])
        pre = sb("pre", [P, B])
        att = ctx.enter_context(ExitStack())

        def sba(name, shape, dt=F32):
            return att.enter_context(nc.sbuf_tensor(name, shape, dt))

        wz, wh = sb("wz", [P, D]), sb("wh", [P, D])
        wq, wk, wv, wo = (sb(n, [P, D]) for n in ("wq", "wk", "wv", "wo"))
        wx2, wh2 = sb("wx2", [P, D]), sb("wh2", [P, D])
        cols = sb("cols", [P, 6])
        bv_bc = sb("bv_bc", [P, D])
        leak = sb("leak", [P, 1])
        relk = sb("relk", [P, REL])
        OT1 = sb("OT1", [P, B, T])
        QT = sba("QT", [P, T, B])
        KT = sba("KT", [P, B, T])
        V9 = sba("V9", [P, B, H, DH + 1])
        relv = sba("relv", [P, T, DH])
        relv9 = sba("relv9", [P, T, DH + 1])
        proj = ctx.enter_context(ExitStack())
        hs = proj.enter_context(nc.sbuf_tensor("hs", [P, T + 1, B], F32))

        ps = [ctx.enter_context(nc.psum_tensor(f"bank{i}", [P, BANK], F32)) for i in range(8)]

        s_scan_in = sem("scan_inputs_loaded")
        s_att_in = sem("attention_inputs_loaded")
        s_leak = sem("leak_ready")
        s_gpre = sem("gate_sums_ready")
        s_gate = sem("gate_ready")
        s_upd = sem("gated_input_ready")
        s_pre = sem("tanh_input_ready")
        s_h = sem("state_ready")
        s_proj = sem("projection_ready")
        s_qcp = sem("queries_copied")
        s_kcp = sem("keys_copied")
        s_vcp = sem("values_copied")
        s_v9 = sem("ones_columns_ready")

        with nc.Block() as block:
            @block.sync
            def _(sp):
                for dst, src in ((wz[:], a["wz"]), (wh[:], a["wh"]), (hs[:, 0, :], a["condT"]),
                                 (cols[:], a["cols"]), (xT[:], a["xT"])):
                    sp.dma_start(dst, src).then_inc(s_scan_in, 16)
                for dst, src in ((wq[:], a["wq"]), (wk[:], a["wk"]), (wv[:], a["wv"]), (wo[:], a["wo"]),
                                 (wx2[:], a["wx2"]), (wh2[:], a["wh2"]), (hmask[:], a["hmask"]),
                                 (ident[:], a["ident"]), (bv_bc[:], a["bv"].partition_broadcast(P))):
                    sp.dma_start(dst, src).then_inc(s_att_in, 16)
                for h in range(H):
                    sp.dma_start(relk[h * DH:(h + 1) * DH, :], a["relk"]).then_inc(s_att_in, 16)
                win = bass.AP(a["relv"].tensor, 0, [[DH, P], [1, T * DH]])
                sp.dma_start(relv[:].rearrange("p q d -> p (q d)"), win).then_inc(s_att_in, 16)

            @block.tensor
            def _(pe):
                pe.wait_ge(s_scan_in, 16 * 5)
                with pe.Fori(0, T // 2) as i:
                    for r in range(2):
                        t = i * 2 + r
                        pe.matmul(ps[r][:, 0:B], wz[:], xT[:, bass.ds(t, 1), :], start=True, stop=False)
                        pe.wait_ge(s_h, t + 1)
                        pe.matmul(ps[r][:, 0:B], wh[:], hs[:, bass.ds(t, 1), :], start=False, stop=True)\
                          .then_inc(s_gpre, 1)

            @block.scalar
            def _(act):
                act.sem_inc(s_h, 1)
                act.wait_ge(s_scan_in, 16 * 5)
                with act.Fori(0, T // 2) as i:
                    for r in range(2):
                        t = i * 2 + r
                        act.wait_ge(s_gpre, t + 1)
                        act.activation(gate[:], ps[r][:, 0:B], ACT.Sigmoid, bias=cols[:, 0:1]).then_inc(s_gate, 1)
                        act.wait_ge(s_pre, t + 1)
                        act.activation(hs[:, bass.ds(t + 1, 1), :], pre[:].unsqueeze(1), ACT.Tanh).then_inc(s_h, 1)

            @block.vector
            def _(dve):
                dve.wait_ge(s_scan_in, 16 * 5)
                dve.tensor_scalar(leak[:], cols[:, 1:2], -1.0, 1.0, ALU.mult, ALU.add).then_inc(s_leak, 1)
                dve.wait_ge(s_leak, 1)
                with dve.Fori(0, T) as t:
                    dve.wait_ge(s_gate, t + 1)
                    dve.tensor_tensor(upd[:].unsqueeze(1), gate[:].unsqueeze(1), xT[:, bass.ds(t, 1), :], ALU.mult)\
                       .then_inc(s_upd, 1)
                    dve.wait_ge(s_upd, t + 1)
                    dve.scalar_tensor_tensor(out=pre[:].unsqueeze(1), in0=hs[:, bass.ds(t, 1), :], scalar=leak[:, 0:1],
                                             in1=upd[:].unsqueeze(1), op0=ALU.mult, op1=ALU.add).then_inc(s_pre, 1)

        with nc.Block() as block:
            NATT = 16 * (9 + H + 1)

            @block.tensor
            def _(pe):
                pe.wait_ge(s_att_in, NATT)
                pe.wait_ge(s_h, T + 1)
                with pe.Fori(0, NCH) as c:
                    pe.wait_ge(s_qcp, c + 1)
                    pe.wait_ge(s_kcp, c + 1)
                    rhs = hs[:, bass.ds(c * TC + 1, TC), :]
                    pe.matmul(ps[0][:], wq[:], rhs, start=True, stop=True).then_inc(s_proj, 1)
                    pe.matmul(ps[1][:], wk[:], rhs, start=True, stop=True).then_inc(s_proj, 1)
                for g in range(B // 4):
                    if g >= 4:
                        pe.wait_ge(s_vcp, g - 3)
                    for j in range(4):
                        mm = pe.matmul(ps[2 + g % 4][:, j * D:(j + 1) * D], hs[:, 1:T + 1, 4 * g + j], wv[:],
                                       start=True, stop=True)
                    mm.then_inc(s_proj, 1)

            @block.scalar
            def _(act):
                act.sem_inc(s_kcp, 1)
                act.wait_ge(s_att_in, NATT)
                with act.Fori(0, NCH) as c:
                    act.wait_ge(s_proj, c * 2 + 2)
                    act.activation(KT[:, :, bass.ds(c * TC, TC)].rearrange("p b t -> p t b"),
                                   ps[1][:].rearrange("p (t b) -> p t b", b=B), ACT.Identity, bias=cols[:, 3:4])\
                       .then_inc(s_kcp, 1)

            @block.vector
            def _(dve):
                dve.sem_inc(s_qcp, 1)
                dve.wait_ge(s_att_in, NATT)
                dve.memset(V9[:, :, :, DH:], 1.0).then_inc(s_v9, 1)
                dve.memset(relv9[:, :, DH:], 1.0).then_inc(s_v9, 1)
                dve.tensor_copy(relv9[:, :, 0:DH], relv[:]).then_inc(s_v9, 1)
                with dve.Fori(0, NCH) as c:
                    dve.wait_ge(s_proj, c * 2 + 1)
                    dve.tensor_scalar(QT[:, bass.ds(c * TC, TC), :], ps[0][:].rearrange("p (t b) -> p t b", b=B),
                                      cols[:, 2:3], None, ALU.add).then_inc(s_qcp, 1)
                for g in range(B // 4):
                    dve.wait_ge(s_proj, 2 * NCH + g + 1)
                    dve.tensor_tensor(V9[:, 4 * g:4 * g + 4, :, 0:DH],
                                      ps[2 + g % 4][:].rearrange("p (b h d) -> p b h d", b=4, h=H),
                                      bv_bc[:].rearrange("p (h d) -> p h d", h=H).unsqueeze(1)
                                      .broadcast_to([P, 4, H, DH]), ALU.add).then_inc(s_vcp, 1)

        proj.close()

        with ExitStack() as st3:
            qm = [st3.enter_context(nc.sbuf_tensor(f"qm{i}", [P, QS, QUAD, B], F32)) for i in range(2)]
            seg = [st3.enter_context(nc.sbuf_tensor(f"seg{i}", [P, SEG], F32)) for i in range(2)]
            SETS = QS // 4
            stage = [st3.enter_context(nc.sbuf_tensor(f"s2stage{i}", [P, NHG, BANK], F32)) for i in range(SETS)]
            s_qm = sem("masked_queries_ready")
            s_s2 = sem("relative_scores_ready")
            s_s2a = sem("relative_scores_copied_scalar")
            s_s2v = sem("relative_scores_copied_vector")
            s_s2w = [sem(f"relative_scores_written{i}") for i in range(SETS)]
            NBODY = T // QS
            s2_out = s2_dram.rearrange("(g n) q k -> n g q k", g=NHG)
            with nc.Block() as block:
                @block.gpsimd
                def _(pool):
                    def body(it, r):
                        pool.tensor_copy(seg[r][:], relk[:, bass.ds((T - QS) - it * QS, SEG)])
                        pool.tensor_tensor(qm[r][:], QT[:, bass.ds(it * QS, QS), :].unsqueeze(2)
                                           .broadcast_to([P, QS, QUAD, B]),
                                           hmask[:].unsqueeze(1).unsqueeze(3).broadcast_to([P, QS, QUAD, B]),
                                           ALU.mult).then_inc(s_qm, 1)

                    body(0, 0)
                    body(1, 1)
                    with pool.Fori(1, NBODY // 2) as i:
                        for r in range(2):
                            pool.wait_ge(s_s2, (i * 2 + (r - 1)) * SETS)
                            body(i * 2 + r, r)

                @block.tensor
                def _(pe):
                    with pe.Fori(0, NBODY // 2) as i:
                        for r in range(2):
                            it = i * 2 + r
                            pe.wait_ge(s_qm, it + 1)
                            for s in range(SETS):
                                pe.wait_ge(s_s2a, it * SETS + max(s - 1, 0) + 1)
                                pe.wait_ge(s_s2v, it * SETS + max(s - 1, 0) + 1)
                                for j in range(4 * s, 4 * s + 4):
                                    for hg in range(NHG):
                                        rows = slice(32 * hg, 32 * hg + 32)
                                        mm = pe.matmul(ps[4 * (s % 2) + hg][:, (j % 4) * T:(j % 4 + 1) * T],
                                                       qm[r][rows, j, :, :], seg[r][rows, QS - 1 - j:QS - 1 - j + T],
                                                       start=True, stop=True)
                                mm.then_inc(s_s2, 1)

                @block.scalar
                def _(act):
                    act.sem_inc(s_s2a, 1)
                    with act.Fori(0, NBODY) as it:
                        for s in range(SETS):
                            act.wait_ge(s_s2, it * SETS + s + 1)
                            act.wait_ge(s_s2w[s], it * 16 + 16)
                            for hg in (0, 1):
                                op = act.activation(stage[s][:, hg, :], ps[4 * (s % 2) + hg][:], ACT.Copy)
                            op.then_inc(s_s2a, 1)

                @block.vector
                def _(dve):
                    dve.sem_inc(s_s2v, 1)
                    with dve.Fori(0, NBODY) as it:
                        for s in range(SETS):
                            dve.wait_ge(s_s2, it * SETS + s + 1)
                            dve.wait_ge(s_s2w[s], it * 16 + 16)
                            for hg in (2, 3):
                                op = dve.tensor_copy(stage[s][:, hg, :], ps[4 * (s % 2) + hg][:])
                            op.then_inc(s_s2v, 1)

                @block.sync
                def _(sp):
                    for s in range(SETS):
                        sp.sem_inc(s_s2w[s], 16)
                    with sp.Fori(0, NBODY) as it:
                        for s in range(SETS):
                            sp.wait_ge(s_s2a, it * SETS + s + 2)
                            sp.wait_ge(s_s2v, it * SETS + s + 2)
                            sp.dma_start(s2_out[:, :, bass.ds(it * QS + 4 * s, 4), :],
                                         stage[s][:].rearrange("p g (q k) -> p g q k", k=T)).then_inc(s_s2w[s], 16)
                    for s in range(SETS):
                        sp.wait_ge(s_s2w[s], 16 * NBODY + 16)

        with ExitStack() as st4:
            def sb4(name, shape, dt=F32):
                return st4.enter_context(nc.sbuf_tensor(name, shape, dt))

            HH = H // 2
            UW = HH * T
            NU = 2 * GB
            RING = 4
            LAG = 3
            PT = sb4("PT", [P, P, T])
            qb = [sb4(f"qb{i}", [P, QUAD, T]) for i in range(2)]
            kb = [sb4(f"kb{i}", [P, T]) for i in range(2)]
            s2t = [sb4(f"s2t{i}", [P, HH, T]) for i in range(RING)]
            sc = [sb4(f"sc{i}", [P, HH, T]) for i in range(RING)]
            mx = [sb4(f"mx{i}", [P, HH]) for i in range(RING)]
            w1n = [sb4(f"w1n{i}", [P, H, DH]) for i in range(2)]
            rc1 = [sb4(f"rc1_{i}", [P, H]) for i in range(2)]
            QC = 32
            NQC = T // QC
            w2n = [sb4(f"w2n{i}", [P, QC, DH]) for i in range(2)]
            w2s = [sb4(f"w2s{i}", [P, P]) for i in range(2)]
            rc2 = [sb4(f"rc2_{i}", [P, QC]) for i in range(2)]

            s_qk = sem("batch_queries_keys_ready")
            s_s1 = sem("content_scores_ready")
            s_s2l = [sem(f"relative_scores_loaded{i}") for i in range(RING)]
            s_add = sem("scores_summed")
            s_max = sem("row_maxima_ready")
            s_sub = sem("maxima_subtracted")
            s_exp = sem("exp_ready")
            s_tr = sem("exp_transposed")
            s_pta = sem("transposed_copied_scalar")
            s_ptv = sem("transposed_copied_vector")
            s_w1 = sem("value_product_ready")
            s_rc1 = sem("value_reciprocals_ready")
            s_w1n = sem("value_product_normalised")
            s_w1t = sem("value_product_transposed")
            s_w1c = sem("value_product_stored")
            s_w2 = sem("relative_value_product_ready")
            s_rc2 = sem("relative_value_reciprocals_ready")
            s_w2n = sem("relative_value_product_normalised")
            s_w2t = sem("relative_value_product_transposed")
            s_w2c = sem("relative_value_product_copied")
            s_w2d = [sem(f"relative_value_product_written{i}") for i in range(2)]
            s2_in = s2_dram.rearrange("(h p r) q k -> q h p r k", h=H, r=2)

            with nc.Block() as block:
                @block.sync
                def _(sp):
                    with sp.Fori(0, 2) as gp:
                        with sp.Fori(0, 2) as gm:
                            g = gp * 2 + gm
                            for u in range(NU):
                                sp.wait_ge(s_add, g * NU + max(u - RING + 1, 0) + 1)
                                half = u % 2
                                src = s2_in[:, bass.ds(gm * GB + u // 2, 1), half * HH:(half + 1) * HH,
                                            bass.ds(gp, 1), :]
                                sp.dma_start(s2t[u % RING][:], src.rearrange("q a p r k -> q (a p r) k"))\
                                  .then_inc(s_s2l[u % RING], 16)

                @block.gpsimd
                def _(pool):
                    with pool.Fori(0, NG) as g:
                        def batch_operands(bl):
                            pool.wait_ge(s_s1, g * NU + 2 * max(bl - 1, 0) + 1)
                            pool.tensor_tensor(qb[bl % 2][:],
                                               QT[:, :, bass.ds(g * GB + bl, 1)].rearrange("p t b -> p b t")
                                               .broadcast_to([P, QUAD, T]),
                                               hmask[:].unsqueeze(2).broadcast_to([P, QUAD, T]), ALU.mult)
                            pool.tensor_copy(kb[bl % 2][:].unsqueeze(1), KT[:, bass.ds(g * GB + bl, 1), :])\
                                .then_inc(s_qk, 1)

                        batch_operands(0)
                        batch_operands(1)
                        for u in range(NU):
                            pool.wait_ge(s_max, g * NU + u + 1)
                            pool.tensor_tensor(sc[u % RING][:], sc[u % RING][:],
                                               mx[u % RING][:].unsqueeze(2).broadcast_to([P, HH, T]), ALU.subtract)\
                                .then_inc(s_sub, 1)
                            if u % 2 and (u + 1) // 2 + 1 < GB:
                                batch_operands((u + 1) // 2 + 1)

                def w1_turn(pe, g, bl):
                    pe.wait_ge(s_w1n, g * GB + bl + 2)
                    if bl == 0:
                        pe.wait_ge(s_w2n, g * NQC + 1)
                    pe.wait_ge(s_w1c, g * GB + bl + 1)
                    pe.transpose(ps[7][:, 0:T], w1n[bl % 2][:].rearrange("p h d -> p (h d)"), ident[:])\
                      .then_inc(s_w1t, 1)

                @block.tensor
                def _(pe):
                    pe.sem_inc(s_s1, 1)
                    pe.sem_inc(s_w2, 1)
                    with pe.Fori(0, NG) as g:
                        for u in range(NU + 5):
                            if u < NU:
                                bl, half = u // 2, u % 2
                                pe.wait_ge(s_qk, g * GB + bl + 1)
                                if u >= 2:
                                    pe.wait_ge(s_add, g * NU + u)
                                for ho in range(QUAD):
                                    for s in range(2):
                                        rows = slice(32 * (2 * half + s), 32 * (2 * half + s) + 32)
                                        mm = pe.matmul(ps[2 * (u % 2) + s][:, ho * T:(ho + 1) * T],
                                                       qb[bl % 2][rows, ho, :], kb[bl % 2][rows, :],
                                                       start=True, stop=True)
                                mm.then_inc(s_s1, 1)
                            if u >= 5 and u % 2:
                                bl = (u - 5) // 2
                                pe.wait_ge(s_pta, g * NU + 2 * bl + 2 + 1)
                                pe.wait_ge(s_ptv, g * NU + 2 * bl + 2 + 1)
                                pe.wait_ge(s_w1n, g * GB + bl + 1)
                                for h in range(H):
                                    mm = pe.matmul(ps[6][:, h * (DH + 1):(h + 1) * (DH + 1)], PT[:, bl * H + h, :],
                                                   V9[:, bass.ds(g * GB + bl, 1), h, :], start=True, stop=True)
                                mm.then_inc(s_w1, 1)
                            if LAG <= u < NU + LAG:
                                v = u - LAG
                                pe.wait_ge(s_exp, g * NU + v + 1)
                                for s in range(2):
                                    pe.wait_ge(s_ptv if s else s_pta, g * NU + v + 1)
                                    if v == 0:
                                        pe.wait_ge(s_w2c, g * 2 * NQC + 1)
                                    for j in range(4):
                                        mm = pe.transpose(ps[4 + s][:, j * T:(j + 1) * T],
                                                          sc[v % RING][:, 4 * s + j, :], ident[:])
                                    mm.then_inc(s_tr, 1)
                            if u >= 6 and u % 2 == 0:
                                w1_turn(pe, g, (u - 6) // 2)
                        for c in range(NQC + 1):
                            if c < NQC:
                                if c == 0:
                                    pe.wait_ge(s_w1c, g * GB + GB + 1)
                                elif c >= 2:
                                    pe.wait_ge(s_w2n, g * NQC + c)
                                for j in range(QC):
                                    q = QC * c + j
                                    mm = pe.matmul(ps[7 - c % 2][:, j * (DH + 1):(j + 1) * (DH + 1)], PT[:, :, q],
                                                   relv9[:, T - 1 - q, :], start=True, stop=True)
                                mm.then_inc(s_w2, 1)
                            if c >= 1:
                                pe.wait_ge(s_w2n, g * NQC + c + 1)
                                for x in range(2):
                                    n = 2 * (c - 1) + x
                                    if n >= 2:
                                        pe.wait_ge(s_w2c, g * 2 * NQC + n)
                                    pe.transpose(ps[4 + x][:, 0:P],
                                                 w2n[(c - 1) % 2][:, x * QC // 2:(x + 1) * QC // 2, :]
                                                 .rearrange("p q d -> p (q d)"), ident[:]).then_inc(s_w2t, 1)

                @block.vector
                def _(dve):
                    dve.sem_inc(s_add, 1)
                    dve.sem_inc(s_w1n, 1)
                    dve.sem_inc(s_ptv, 1)
                    dve.sem_inc(s_w2n, 1)
                    with dve.Fori(0, NG) as g:
                        for u in range(NU + 5):
                            if u < NU:
                                r = u % RING
                                dve.wait_ge(s_s1, g * NU + u + 2)
                                dve.wait_ge(s_s2l[r], (g * (NU // RING) + u // RING + 1) * 16)
                                if u >= RING:
                                    dve.wait_ge(s_tr, (g * NU + u - RING + 1) * 2)
                                for s in range(2):
                                    op = dve.tensor_tensor(sc[r][:, 4 * s:4 * s + 4, :],
                                                           ps[2 * (u % 2) + s][:].rearrange("p (h k) -> p h k", k=T),
                                                           s2t[r][:, 4 * s:4 * s + 4, :], ALU.add)
                                op.then_inc(s_add, 1)
                                dve.wait_ge(s_add, g * NU + u + 2)
                                dve.tensor_reduce(mx[r][:], sc[r][:], AX.X, ALU.max).then_inc(s_max, 1)
                            if LAG <= u < NU + LAG:
                                v = u - LAG
                                dve.wait_ge(s_tr, (g * NU + v) * 2 + 2)
                                if v == 0:
                                    dve.wait_ge(s_w2, g * NQC + 1)
                                dve.tensor_copy(PT[:, v * HH + 4:v * HH + 8, :],
                                                ps[5][:].rearrange("p (h q) -> p h q", q=T)).then_inc(s_ptv, 1)
                            if u >= 5 and u % 2:
                                bl = (u - 5) // 2
                                w1v = ps[6][:, 0:H * (DH + 1)].rearrange("p (h d) -> p h d", d=DH + 1)
                                dve.wait_ge(s_w1, g * GB + bl + 1)
                                dve.reciprocal(rc1[bl % 2][:].unsqueeze(2), w1v[:, :, DH:]).then_inc(s_rc1, 1)
                                dve.wait_ge(s_rc1, g * GB + bl + 1)
                                if bl >= 2:
                                    dve.wait_ge(s_w1t, g * GB + bl - 1)
                                dve.tensor_tensor(w1n[bl % 2][:], w1v[:, :, 0:DH],
                                                  rc1[bl % 2][:].unsqueeze(2).broadcast_to([P, H, DH]), ALU.mult)\
                                   .then_inc(s_w1n, 1)
                        for c in range(NQC):
                            w2v = ps[7 - c % 2][:, 0:QC * (DH + 1)].rearrange("p (q d) -> p q d", d=DH + 1)
                            dve.wait_ge(s_w2, g * NQC + c + 2)
                            dve.reciprocal(rc2[c % 2][:].unsqueeze(2), w2v[:, :, DH:]).then_inc(s_rc2, 1)
                            dve.wait_ge(s_rc2, g * NQC + c + 1)
                            if c >= 2:
                                dve.wait_ge(s_w2t, (g * NQC + c - 1) * 2)
                            dve.tensor_tensor(w2n[c % 2][:], w2v[:, :, 0:DH],
                                              rc2[c % 2][:].unsqueeze(2).broadcast_to([P, QC, DH]), ALU.mult)\
                               .then_inc(s_w2n, 1)

                @block.scalar
                def _(act):
                    act.sem_inc(s_pta, 1)
                    act.sem_inc(s_w2c, 1)
                    act.sem_inc(s_w1c, 1)
                    act.sem_inc(s_w2d[0], 16)
                    act.sem_inc(s_w2d[1], 16)
                    with act.Fori(0, NG) as g:
                        for u in range(NU + 5):
                            if u < NU:
                                act.wait_ge(s_sub, g * NU + u + 1)
                                act.activation(sc[u % RING][:], sc[u % RING][:], ACT.Exp, scale=DH ** -0.5)\
                                   .then_inc(s_exp, 1)
                            if LAG <= u < NU + LAG:
                                v = u - LAG
                                act.wait_ge(s_tr, (g * NU + v) * 2 + 1)
                                if v == 0:
                                    act.wait_ge(s_w2, g * NQC + 1)
                                act.activation(PT[:, v * HH:v * HH + 4, :],
                                               ps[4][:].rearrange("p (h q) -> p h q", q=T), ACT.Copy)\
                                   .then_inc(s_pta, 1)
                            if u >= 6 and u % 2 == 0:
                                bl = (u - 6) // 2
                                act.wait_ge(s_w1t, g * GB + bl + 1)
                                act.activation(OT1[:, bass.ds(g * GB + bl, 1), :], ps[7][:, 0:T].unsqueeze(1), ACT.Copy)\
                                   .then_inc(s_w1c, 1)
                        for n in range(2 * NQC):
                            act.wait_ge(s_w2t, g * 2 * NQC + n + 1)
                            act.wait_ge(s_w2d[n % 2], (g * NQC + n // 2) * 16 + 16)
                            act.activation(w2s[n % 2][:], ps[4 + n % 2][:, 0:P], ACT.Copy).then_inc(s_w2c, 1)
                            act.wait_ge(s_w2c, g * 2 * NQC + n + 2)
                            act.dma_start(w2_dram[n * P:(n + 1) * P, bass.ds(g * P, P)], w2s[n % 2][:])\
                               .then_inc(s_w2d[n % 2], 16)
                    for r in range(2):
                        act.wait_ge(s_w2d[r], 16 * NG * NQC + 16)
        att.close()

        with ExitStack() as st5:
            OT2 = st5.enter_context(nc.sbuf_tensor("OT2", [P, T, B], F32))
            s_ot2 = sem("relative_value_outputs_loaded")
            s_y = sem("output_projection_ready")
            s_x1 = sem("residual_ready")
            with nc.Block() as block:
                w2_in = w2_dram.rearrange("(q d) (h b) -> h d q b", d=DH, b=B)

                @block.sync
                def _(sp):
                    for h in range(0, H, 2):
                        sp.dma_start(OT2[h * DH:(h + 1) * DH, :, :], w2_in[h]).then_inc(s_ot2, 16)

                @block.scalar
                def _(act):
                    for h in range(1, H, 2):
                        act.dma_start(OT2[h * DH:(h + 1) * DH, :, :], w2_in[h]).then_inc(s_ot2, 16)

                @block.tensor
                def _(pe):
                    pe.wait_ge(s_ot2, 16 * H)
                    for c in range(NCH):
                        ts = slice(c * TC, (c + 1) * TC)
                        if c >= 2:
                            pe.wait_ge(s_x1, c - 1)
                        pe.matmul(ps[c % 2][:], wo[:], OT1[:, :, ts].rearrange("p b t -> p t b"), start=True, stop=False)
                        pe.matmul(ps[c % 2][:], wo[:], OT2[:, ts, :], start=False, stop=True).then_inc(s_y, 1)

                @block.vector
                def _(dve):
                    for c in range(NCH):
                        ts = slice(c * TC, (c + 1) * TC)
                        dve.wait_ge(s_y, c + 1)
                        dve.scalar_tensor_tensor(out=xT[:, ts, :].rearrange("p t b -> p (t b)"), in0=ps[c % 2][:],
                                                 scalar=cols[:, 4:5], in1=xT[:, ts, :].rearrange("p t b -> p (t b)"),
                                                 op0=ALU.add, op1=ALU.add).then_inc(s_x1, 1)

        h2 = sb("h2", [P, T + 1, B])
        w1T = sb("w1T", [P, E, FF])
        w2T = sb("w2T", [P, E, FC, D])
        b1c = sb("b1c", [P, E, FC])
        b2r = sb("b2r", [E, D])
        rwT = sb("rwT", [P, E])
        iota = sb("iota", [P, E])
        s_c2 = sem("scan2_state_loaded")
        s_ffn_in = sem("ffn_inputs_loaded")
        s_r = sem("scan2_sums_ready")
        s_h2 = sem("scan2_state_ready")
        with nc.Block() as block:
            @block.sync
            def _(sp):
                sp.dma_start(h2[:, 0, :], a["condT"]).then_inc(s_c2, 16)
                for dst, src in ((w1T[:], a["w1T"]), (w2T[:], a["w2T"]), (b1c[:], a["b1c"]), (b2r[:], a["b2"]),
                                 (rwT[:], a["rwT"]), (iota[:], a["iota"].partition_broadcast(P))):
                    sp.dma_start(dst, src).then_inc(s_ffn_in, 16)

            @block.tensor
            def _(pe):
                pe.wait_ge(s_c2, 16)
                with pe.Fori(0, T // 2) as i:
                    for r in range(2):
                        t = i * 2 + r
                        pe.matmul(ps[r][:, 0:B], wx2[:], xT[:, bass.ds(t, 1), :], start=True, stop=False)
                        pe.wait_ge(s_h2, t + 1)
                        pe.matmul(ps[r][:, 0:B], wh2[:], h2[:, bass.ds(t, 1), :], start=False, stop=True)\
                          .then_inc(s_r, 1)

            @block.scalar
            def _(act):
                act.sem_inc(s_h2, 1)
                act.wait_ge(s_c2, 16)
                with act.Fori(0, T // 2) as i:
                    for r in range(2):
                        t = i * 2 + r
                        act.wait_ge(s_r, t + 1)
                        act.activation(h2[:, bass.ds(t + 1, 1), :], ps[r][:, 0:B].unsqueeze(1), ACT.Tanh,
                                       bias=cols[:, 5:6]).then_inc(s_h2, 1)

        xc = [sb(f"xc{i}", [P, BANK]) for i in range(2)]
        rc = [sb(f"resc{i}", [P, BANK]) for i in range(2)]
        hid = [sb(f"hid{i}", [P, FC, BANK]) for i in range(2)]
        top = sb("top", [P, JT, 8])
        topi = sb("topi", [P, JT, 8], U32)
        topf = sb("topf", [P, JT, 8])
        lg = sb("lg", [P, JT, E])
        lgc = sb("lgc", [P, JT, E])
        ex = sb("ex", [P, JT, E])
        small = sb("small", [P, 4, JT])
        w01 = sb("w01", [P, JT, 2])
        sel = sb("sel", [P, 2, JT, E])
        cw = sb("cw", [P, JT, E])
        cwT = sb("cwT", [E, JT, P])
        acc = [sb(f"acc{i}", [P, JT, D]) for i in range(2)]
        s_xc = sem("chunk_operands_ready")
        s_lg = sem("logits_ready")
        s_v = sem("vector_chain")
        s_ea = sem("router_shift_ready")
        s_eb = sem("router_exp_ready")
        s_cw = sem("combine_weights_ready")
        s_cwt = sem("combine_weights_transposed")
        s_cwc = sem("combine_weights_copied")
        s_b2 = sem("start_rows_ready")
        s_acc0 = sem("start_rows_copied")
        s_up = sem("hidden_sums_ready")
        s_hid = sem("hidden_ready")
        s_dn = sem("expert_rows_ready")
        s_mix = sem("expert_rows_added")
        s_out = [sem(f"output_written{i}") for i in range(2)]
        with nc.Block() as block:
            @block.gpsimd
            def _(pool):
                def operands(c, r):
                    pool.tensor_copy(xc[r][:].rearrange("p (t b) -> p t b", b=B), h2[:, bass.ds(c * TC + 1, TC), :])
                    pool.tensor_copy(rc[r][:].rearrange("p (t b) -> p t b", b=B), xT[:, bass.ds(c * TC, TC), :])\
                        .then_inc(s_xc, 1)

                operands(0, 0)
                operands(1, 1)
                with pool.Fori(1, NCH // 2) as i:
                    for r in range(2):
                        pool.wait_ge(s_mix, (i * 2 + (r - 1)) * E + 1)
                        operands(i * 2 + r, r)

            @block.tensor
            def _(pe):
                pe.sem_inc(s_dn, 1)
                pe.wait_ge(s_ffn_in, 16 * 6)
                with pe.Fori(0, NCH // 2) as i:
                    for r in range(2):
                        c = i * 2 + r
                        pe.wait_ge(s_xc, c + 1)
                        pe.wait_ge(s_cwc, c + 1)
                        for j in range(JT):
                            mm = pe.matmul(ps[6][:, j * E:(j + 1) * E], xc[r][:, j * P:(j + 1) * P], rwT[:],
                                           start=True, stop=True)
                        mm.then_inc(s_lg, 1)

                        def up(e):
                            for f in range(FC):
                                pe.wait_ge(s_hid, (c * E + e) * FC - (FC - 1 - f if e else 0) + 1)
                                pe.matmul(ps[f][:], w1T[:, e, f * P:(f + 1) * P], xc[r][:], start=True, stop=True)\
                                  .then_inc(s_up, 1)

                        def start_rows():
                            pe.wait_ge(s_cw, c + 1)
                            for j in range(JT):
                                mm = pe.transpose(ps[6][0:E, j * P:(j + 1) * P], cw[:, j, :], ident[:])
                            mm.then_inc(s_cwt, 1)
                            pe.wait_ge(s_cwc, c + 2)
                            pe.wait_ge(s_acc0, c + 1)
                            for j in range(JT):
                                pe.matmul(ps[7][:, j * D:(j + 1) * D], rc[r][:, j * P:(j + 1) * P], ident[:],
                                          start=True, stop=False)
                                mm = pe.matmul(ps[7][:, j * D:(j + 1) * D], cwT[:, j, :], b2r[:],
                                               start=False, stop=True)
                            mm.then_inc(s_b2, 1)

                        def down(e):
                            n = c * E + e
                            pe.wait_ge(s_hid, (n + 1) * FC + 1)
                            pe.wait_ge(s_mix, n - min(e, 1) + 1)
                            for j in range(JT):
                                for f in range(FC):
                                    mm = pe.matmul(ps[4 + e % 2][:, j * D:(j + 1) * D],
                                                   hid[e % 2][:, f, j * P:(j + 1) * P], w2T[:, e, f, :],
                                                   start=(f == 0), stop=(f == FC - 1))
                            mm.then_inc(s_dn, 1)

                        up(0)
                        for e in range(E):
                            if e + 1 < E:
                                up(e + 1)
                            if e == 0:
                                start_rows()
                            down(e)

            @block.scalar
            def _(act):
                act.sem_inc(s_hid, 1)
                act.wait_ge(s_ffn_in, 16 * 6)
                with act.Fori(0, NCH) as c:
                    act.wait_ge(s_ea, c + 1)
                    act.activation(ex[:], lg[:], ACT.Exp).then_inc(s_eb, 1)
                    for e in range(E):
                        n = c * E + e
                        act.wait_ge(s_dn, n - min(e, 1) + 1)
                        for f in range(FC):
                            act.wait_ge(s_up, n * FC + f + 1)
                            act.activation(hid[e % 2][:, f, :], ps[f][:], ACT.Gelu, bias=b1c[:, e, f:f + 1])\
                               .then_inc(s_hid, 1)

            @block.vector
            def _(dve):
                dve.sem_inc(s_cwc, 1)
                dve.sem_inc(s_acc0, 1)
                dve.sem_inc(s_mix, 1)
                dve.wait_ge(s_ffn_in, 16 * 6)
                STEPS = 10
                with dve.Fori(0, NCH // 2) as i:
                    for r in range(2):
                        c = i * 2 + r
                        base = c * STEPS
                        k = [0]

                        def link(op):
                            k[0] += 1
                            op.then_inc(s_v, 1)
                            dve.wait_ge(s_v, base + k[0])

                        dve.wait_ge(s_lg, c + 1)
                        logits = ps[6][:, 0:JT * E].rearrange("p (j e) -> p j e", e=E)
                        link(dve.tensor_copy(lgc[:], logits))
                        dve.tensor_reduce(small[:, 0, :], lgc[:], AX.X, ALU.max)
                        for j in range(JT):
                            op = dve.max(top[:, j, :], lgc[:, j, :])
                        link(op)
                        dve.tensor_tensor(lg[:], lgc[:], small[:, 0, :].unsqueeze(2).broadcast_to([P, JT, E]),
                                          ALU.subtract).then_inc(s_ea, 1)
                        for j in range(JT):
                            op = dve.max_index(topi[:, j, :], top[:, j, :], lgc[:, j, :])
                        link(op)
                        link(dve.tensor_copy(topf[:], topi[:]))
                        dve.wait_ge(s_eb, c + 1)
                        dve.tensor_reduce(small[:, 0, :], ex[:], AX.X, ALU.add)
                        for x in range(2):
                            op = dve.tensor_tensor(sel[:, x], iota[:].unsqueeze(1).broadcast_to([P, JT, E]),
                                                   topf[:, :, x:x + 1].broadcast_to([P, JT, E]), ALU.is_equal)
                        link(op)
                        link(dve.tensor_tensor(cw[:], sel[:, 0], sel[:, 1], ALU.add))
                        link(dve.tensor_tensor(cw[:], cw[:], ex[:], ALU.mult))
                        link(dve.tensor_reduce(small[:, 1, :], cw[:], AX.X, ALU.add))
                        link(dve.scalar_tensor_tensor(out=small[:, 2, :], in0=small[:, 0, :], scalar=1e-9,
                                                      in1=small[:, 1, :], op0=ALU.mult, op1=ALU.add))
                        link(dve.reciprocal(small[:, 3, :], small[:, 2, :]))
                        dve.tensor_tensor(cw[:], cw[:], small[:, 3, :].unsqueeze(2).broadcast_to([P, JT, E]),
                                          ALU.mult).then_inc(s_cw, 1)
                        dve.wait_ge(s_cw, c + 1)
                        dve.wait_ge(s_cwt, c + 1)
                        dve.tensor_copy(cwT[:].rearrange("p j t -> p (j t)"), ps[6][0:E, :]).then_inc(s_cwc, 1)
                        dve.wait_ge(s_b2, c + 1)
                        dve.wait_ge(s_out[r], i * 16 + 16)
                        dve.tensor_copy(acc[r][:].rearrange("p j d -> p (j d)"), ps[7][:]).then_inc(s_acc0, 1)
                        dve.wait_ge(s_acc0, c + 2)
                        for e in range(E):
                            dve.wait_ge(s_dn, c * E + e + 2)
                            if e >= 1:
                                dve.wait_ge(s_mix, c * E + e + 1)
                            for j in range(JT):
                                op = dve.scalar_tensor_tensor(out=acc[r][:, j, :],
                                                              in0=ps[4 + e % 2][:, j * D:(j + 1) * D],
                                                              scalar=cw[:, j, e:e + 1], in1=acc[r][:, j, :],
                                                              op0=ALU.mult, op1=ALU.add)
                            op.then_inc(s_mix, 1)
                        assert k[0] == STEPS

            @block.sync
            def _(sp):
                sp.sem_inc(s_out[0], 16)
                sp.sem_inc(s_out[1], 16)
                with sp.Fori(0, NCH // 2) as i:
                    for r in range(2):
                        c = i * 2 + r
                        sp.wait_ge(s_mix, (c + 1) * E + 1)
                        sp.dma_start(a["out"].rearrange("(c j p) d -> c p j d", j=JT, p=P)[bass.ds(c, 1)]
                                     .rearrange("c p j d -> (c p) j d"), acc[r][:]).then_inc(s_out[r], 16)
                for r in range(2):
                    sp.wait_ge(s_out[r], 16 * (NCH // 2) + 16)


def kernel(x, cond_1024, L0_cond_W, L0_cond_b, L0_cond_alpha, L0_attn_Wq, L0_attn_bq, L0_attn_Wk, L0_attn_bk,
           L0_attn_Wv, L0_attn_bv, L0_attn_Wo, L0_attn_bo, L0_attn_rel_k_emb, L0_attn_rel_v_emb,
           L0_cond2_Wx, L0_cond2_Wh, L0_cond2_b, L0_ffn_router_w, L0_ffn_expert_w1, L0_ffn_expert_b1,
           L0_ffn_expert_w2, L0_ffn_expert_b2):
    import numpy as np
    import concourse.bacc as bacc
    from concourse.bass_utils import run_bass_kernel_spmd

    f = np.asarray
    heads = np.arange(P) // DH % QUAD
    arrays = {
        "xT": f(x).transpose(2, 1, 0),
        "condT": f(cond_1024).T,
        "wh": f(L0_cond_W)[:, :D].T, "wz": f(L0_cond_W)[:, D:].T,
        "wq": f(L0_attn_Wq).T, "wk": f(L0_attn_Wk).T, "wv": f(L0_attn_Wv).T, "wo": f(L0_attn_Wo).T,
        "wx2": f(L0_cond2_Wx), "wh2": f(L0_cond2_Wh),
        "cols": np.stack([f(v) for v in (L0_cond_b, L0_cond_alpha, L0_attn_bq, L0_attn_bk, L0_attn_bo,
                                         L0_cond2_b)], axis=1),
        "bv": f(L0_attn_bv),
        "relk": f(L0_attn_rel_k_emb)[REL:0:-1].T,
        "relv": f(L0_attn_rel_v_emb)[REL:0:-1],
        "hmask": (heads[:, None] == np.arange(QUAD)[None, :]).astype(np.float32),
        "ident": np.eye(P, dtype=np.float32),
        "w1T": f(L0_ffn_expert_w1).transpose(2, 0, 1),
        "w2T": f(L0_ffn_expert_w2).reshape(E, D, FC, P).transpose(3, 0, 2, 1),
        "b1c": f(L0_ffn_expert_b1).reshape(E, FC, P).transpose(2, 0, 1),
        "b2": f(L0_ffn_expert_b2),
        "rwT": f(L0_ffn_router_w).T,
        "iota": np.arange(E, dtype=np.float32),
    }
    arrays = {n: np.ascontiguousarray(v) for n, v in arrays.items()}
    nc = bacc.Bacc("TRN2", target_bir_lowering=False, num_devices=1)
    a = {n: nc.dram_tensor(f"in_{n}", v.shape, mybir.dt.from_np(v.dtype), kind="ExternalInput").ap()
         for n, v in arrays.items()}
    a["out"] = nc.dram_tensor("out_rows", (T * B, D), F32, kind="ExternalOutput").ap()
    build(nc, a)
    r = run_bass_kernel_spmd(nc, [{f"in_{n}": v for n, v in arrays.items()}], core_ids=[0])
    return r.results[0]["out_rows"].reshape(T, B, D).transpose(1, 0, 2)
```

```python
from contextlib import ExitStack

import concourse.bass as bass
from concourse import mybir

F32 = mybir.dt.float32
BF16 = mybir.dt.bfloat16
F16 = mybir.dt.float16
U32 = mybir.dt.uint32
ALU = mybir.AluOpType
ACT = mybir.ActivationFunctionType
AX = mybir.AxisListType

P = 128
B = 32
T = 128
D = 128
H = 16
DH = D // H
QUAD = 4
NHG = H // QUAD
BANK = 512
E = 8
FF = 512
FC = FF // P
TC = BANK // B
NCH = T // TC
JT = BANK // P
GB = 8
NG = B // GB
REL = 2 * T - 1
NP = 3
KS = NP * NP * DH



def build(nc, a):
    with ExitStack() as ctx:
        def sb(name, shape, dt=F32):
            return ctx.enter_context(nc.sbuf_tensor(name, shape, dt))

        def sem(name):
            return ctx.enter_context(nc.semaphore(name))

        s2_dram = nc.dram_tensor("s2_scratch", (H * B, T, T), F32).ap()
        w2_dram = nc.dram_tensor("w2_scratch", (T * DH, H * B), F32).ap()
        qtb_dram = nc.dram_tensor("qtb_scratch", (NCH, NP, NP, DH * H, BANK), BF16).ap()
        qbt_dram = nc.dram_tensor("qbt_scratch", (NP, NP, DH * H, B * T), BF16).ap()
        kbt_dram = nc.dram_tensor("kbt_scratch", (NP, NP, DH * H, B * T), BF16).ap()
        rk_dram = nc.dram_tensor("rk_scratch", (NP, NP, DH, REL), BF16).ap()

        ident = sb("ident", [P, P])
        xT = sb("xT", [P, T, B])
        wz, wh = sb("wz", [P, D]), sb("wh", [P, D])
        wq, wk, wv, wo = (sb(n, [P, D]) for n in ("wq", "wk", "wv", "wo"))
        wx2, wh2 = sb("wx2", [P, D]), sb("wh2", [P, D])
        cols = sb("cols", [P, 6])
        bv_bc = sb("bv_bc", [P, D])
        leak = sb("leak", [P, 1])
        gate = sb("gate", [P, B])
        upd = sb("upd", [P, B])
        pre = sb("pre", [P, B])
        hs = sb("hs", [P, T + 1, B])
        OT1 = hs[:, 0:T, :].rearrange("p t b -> p (t b)").rearrange("p (b t) -> p b t", t=T)
        att = ctx.enter_context(ExitStack())

        def sba(name, shape, dt=F32):
            return att.enter_context(nc.sbuf_tensor(name, shape, dt))

        VW = NP * (DH + 1)
        V27 = sba("V27", [P, B, H, NP, DH + 1], BF16)
        relv27 = sba("relv27", [P, T, NP, DH + 1], BF16)
        scan = ctx.enter_context(ExitStack())

        def sbs(name, shape, dt=F32):
            return scan.enter_context(nc.sbuf_tensor(name, shape, dt))

        rk = sbs("rk", [DH, REL])
        rkp = sbs("rkp", [DH, NP, REL], BF16)
        relkS = sbs("relkS", [KS, REL], BF16)
        relv = sbs("relv", [P, T, DH])
        qf = sbs("qf", [P, B, TC])
        kf = sbs("kf", [P, B, TC])
        qp = [sbs(f"qp{i}", [P, NP, BANK], BF16) for i in range(2)]
        qfull = sbs("qfull", [P, NP, B, T], BF16)
        kfull = sbs("kfull", [P, NP, B, T], BF16)
        QS2 = [sbs(f"QS2_{i}", [KS, H, BANK], BF16) for i in range(2)]
        SETS = TC // 4
        stage = [sbs(f"s2stage{i}", [P, NHG, 4, T]) for i in range(SETS)]
        vf = [sbs(f"vf{i}", [P, 4 * H, DH]) for i in range(2)]

        ps = [ctx.enter_context(nc.psum_tensor(f"bank{i}", [P, BANK], F32)) for i in range(8)]

        s_scan_in = sem("scan_inputs_loaded")
        s_rel_in = sem("relative_tables_loaded")
        s_rel = sem("relative_table_chain")
        s_rkp = sem("relative_key_parts_ready")
        s_rkw = sem("relative_key_parts_written")
        s_rks = sem("relative_key_stack_loaded")
        s_att_in = sem("attention_weights_loaded")
        s_leak = sem("leak_ready")
        s_gpre = sem("gate_sums_ready")
        s_gate = sem("gate_ready")
        s_upd = sem("gated_input_ready")
        s_pre = sem("tanh_input_ready")
        s_h = sem("state_ready")
        s_qps = sem("query_sums_ready")
        s_kps = sem("key_sums_ready")
        s_qf = sem("queries_copied")
        s_kf = sem("keys_copied")
        s_pc = sem("parts_chain")
        s_qp = sem("query_parts_ready")
        s_kp = sem("key_parts_ready")
        s_qw = [sem(f"query_parts_written{i}") for i in range(2)]
        s_qs = [sem(f"query_stack_loaded{i}") for i in range(2)]
        s_s2 = sem("relative_scores_ready")
        s_s2c = sem("relative_scores_copied")
        s_s2w = [sem(f"relative_scores_written{i}") for i in range(SETS)]
        s_full = sem("full_parts_written")
        s_vps = sem("value_sums_ready")
        s_vf = sem("values_copied")
        s_vc = sem("value_parts_chain")
        s_pass = sem("gpsimd_wait_passed")
        s_spass = sem("sync_wait_passed")
        s_vp = sem("value_parts_ready")

        s2_out = s2_dram.rearrange("(g n) q k -> n g q k", g=NHG)
        PLINKS = 7
        VG = B // 4

        def macros(eng, step):
            step(0, 0, True, False, False)
            step(0, 1, True, True, False)
            with eng.Fori(1, NCH // 2) as i:
                for r in range(2):
                    step(i, r, True, True, True)
            step(NCH // 2, 0, False, True, True)
            step(NCH // 2, 1, False, False, True)

        with nc.Block() as block:
            @block.sync
            def _(sp):
                for r in range(2):
                    sp.sem_inc(s_qw[r], 16)
                for s in range(SETS):
                    sp.sem_inc(s_s2w[s], 16)
                for dst, src in ((wz[:], a["wz"]), (wh[:], a["wh"]), (hs[:, 0, :], a["condT"]),
                                 (cols[:], a["cols"]), (xT[:], a["xT"])):
                    sp.dma_start(dst, src).then_inc(s_scan_in, 16)
                sp.dma_start(rk[:], a["relk"]).then_inc(s_rel_in, 16)
                win = bass.AP(a["relv"].tensor, 0, [[DH, P], [1, T * DH]])
                sp.dma_start(relv[:].rearrange("p q d -> p (q d)"), win).then_inc(s_rel_in, 16)
                for dst, src in ((wq[:], a["wq"]), (wk[:], a["wk"]), (wv[:], a["wv"]), (wo[:], a["wo"]),
                                 (wx2[:], a["wx2"]), (wh2[:], a["wh2"]),
                                 (ident[:], a["ident"]), (bv_bc[:], a["bv"].partition_broadcast(P))):
                    sp.dma_start(dst, src).then_inc(s_att_in, 16)
                sp.wait_ge(s_rkp, 1)
                for n in range(NP):
                    sp.dma_start(rk_dram[:, n].rearrange("j d x -> d j x"), rkp[:]).then_inc(s_rkw, 16)
                sp.wait_ge(s_rkw, 16 * NP)
                sp.dma_start(relkS[:], rk_dram.rearrange("j i d x -> (j i d) x")).then_inc(s_rks, 16)

                def write_scores(m, s):
                    c = m - 2
                    sp.wait_ge(s_s2c, c * TC + 4 * s + 4 + 4)
                    sp.sem_inc(s_spass, 1)
                    sp.dma_start(s2_out[:, :, bass.ds(c * TC + 4 * s, 4), :], stage[s][:]).then_inc(s_s2w[s], 16)

                def step(i, r, scan_on, proj_on, rel_on):
                    m = i * 2 + r
                    if rel_on:
                        for s in range(SETS - 1):
                            write_scores(m, s)
                    if proj_on:
                        o = 1 - r
                        fill = i if r else i - 1
                        sp.wait_ge(s_qp, m + 1)
                        sp.sem_inc(s_spass, 1)
                        for n in range(NP):
                            sp.dma_start(qtb_dram[bass.ds(m - 1, 1), n].rearrange("c i p x -> (c p) i x"), qp[o][:])\
                              .then_inc(s_qw[o], 16)
                        sp.wait_ge(s_qw[o], fill * (16 * NP) + 16 + 16 * NP)
                        sp.sem_inc(s_spass, 1)
                        if rel_on:
                            sp.wait_ge(s_s2, (m - 2) * TC + 1)
                        sp.sem_inc(s_spass, 1)
                        sp.dma_start(QS2[o][:], qtb_dram[bass.ds(m - 1, 1)].rearrange(
                            "c j i (d h) x -> (c j i d) h x", h=H)).then_inc(s_qs[o], 16)
                    if rel_on:
                        write_scores(m, SETS - 1)

                macros(sp, step)
                sp.wait_ge(s_kp, NCH + 1)
                sp.wait_ge(s_pc, PLINKS * NCH)
                for n in range(NP):
                    sp.dma_start(qbt_dram[n].rearrange("i p x -> p i x"), qfull[:].rearrange("p i b t -> p i (b t)"))\
                      .then_inc(s_full, 16)
                    sp.dma_start(kbt_dram[:, n].rearrange("j p x -> p j x"),
                                 kfull[:].rearrange("p j b t -> p j (b t)")).then_inc(s_full, 16)
                sp.wait_ge(s_full, 32 * NP)
                for s in range(SETS):
                    sp.wait_ge(s_s2w[s], 16 * NCH + 16)

            @block.tensor
            def _(pe):
                pe.sem_inc(s_s2, 1)
                pe.wait_ge(s_scan_in, 16 * 5)

                def project(w, bank, m, lo, n):
                    return pe.matmul(ps[bank][:, lo * B:(lo + n) * B], w[:], hs[:, bass.ds((m - 1) * TC + 1 + lo, n), :],
                                     start=True, stop=True)

                def step(i, r, scan_on, proj_on, rel_on):
                    m = i * 2 + r
                    if proj_on and not rel_on:
                        pe.wait_ge(s_att_in, 16 * 8)
                        pe.wait_ge(s_rks, 16)
                    if proj_on and not scan_on:
                        pe.wait_ge(s_h, T + 1)
                        pe.wait_ge(s_qf, m)
                        project(wq, 2, m, 0, TC).then_inc(s_qps, 1)
                        pe.wait_ge(s_kf, m)
                        project(wk, 3, m, 0, TC).then_inc(s_kps, 1)
                        for g in range(VG):
                            if g >= 2:
                                pe.wait_ge(s_vf, g - 1)
                            for j in range(4):
                                mm = pe.matmul(ps[g % 2][:, j * D:(j + 1) * D], hs[:, 1:T + 1, 4 * g + j], wv[:],
                                               start=True, stop=True)
                            mm.then_inc(s_vps, 1)
                    for j in range(TC):
                        if scan_on:
                            t = m * TC + j
                            pe.matmul(ps[j % 2][:, 0:B], wz[:], xT[:, bass.ds(t, 1), :], start=True, stop=False)
                            pe.wait_ge(s_h, t + 1)
                            pe.matmul(ps[j % 2][:, 0:B], wh[:], hs[:, bass.ds(t, 1), :], start=False, stop=True)\
                              .then_inc(s_gpre, 1)
                            if proj_on and j < 8:
                                if j == 0:
                                    pe.wait_ge(s_qf, m)
                                if j == 4:
                                    pe.wait_ge(s_kf, m)
                                mm = project(wk if j >= 4 else wq, 2 + j // 4, m, 4 * (j % 4), 4)
                                if j % 4 == 3:
                                    mm.then_inc(s_kps if j >= 4 else s_qps, 1)
                        if rel_on:
                            c = m - 2
                            if j == 0:
                                pe.wait_ge(s_qs[r], i * 16)
                            pe.wait_ge(s_s2c, c * TC + j + 1)
                            for g in range(NHG):
                                mm = pe.matmul(ps[4 + j % 4][:, g * T:(g + 1) * T],
                                               QS2[r][:, 4 * g:4 * g + 4, j::TC],
                                               relk_window(c, j), start=True, stop=True)
                            mm.then_inc(s_s2, 1)

                def relk_window(c, j):
                    return relkS[:, bass.ds(c * (-TC) + (T - 1 - j), T)]

                macros(pe, step)

            @block.scalar
            def _(act):
                act.sem_inc(s_h, 1)
                act.sem_inc(s_qf, 1)
                act.sem_inc(s_kf, 1)
                act.preload_act_table_set("sigmoid_and_others")
                act.wait_ge(s_scan_in, 16 * 5)

                def step(i, r, scan_on, proj_on, rel_on):
                    m = i * 2 + r
                    for j in range(TC):
                        if scan_on:
                            t = m * TC + j
                            act.wait_ge(s_gpre, t + 1)
                            act.activation(gate[:], ps[j % 2][:, 0:B], ACT.Sigmoid, bias=cols[:, 0:1]).then_inc(s_gate, 1)
                            act.wait_ge(s_pre, t + 1)
                            act.activation(hs[:, bass.ds(t + 1, 1), :], pre[:].unsqueeze(1), ACT.Tanh).then_inc(s_h, 1)
                        if proj_on and j == 4:
                            act.wait_ge(s_qps, m)
                            act.wait_ge(s_qp, m)
                            act.activation(qf[:].rearrange("p b t -> p t b"), ps[2][:].rearrange("p (t b) -> p t b", b=B), ACT.Identity,
                                           bias=cols[:, 2:3]).then_inc(s_qf, 1)
                        if proj_on and j == 8:
                            act.wait_ge(s_kps, m)
                            act.wait_ge(s_kp, m)
                            act.activation(kf[:].rearrange("p b t -> p t b"),
                                           ps[3][:].rearrange("p (t b) -> p t b", b=B), ACT.Identity,
                                           bias=cols[:, 3:4]).then_inc(s_kf, 1)

                macros(act, step)

            @block.vector
            def _(dve):
                dve.sem_inc(s_s2c, 4)
                dve.wait_ge(s_scan_in, 16 * 5)
                dve.tensor_scalar(leak[:], cols[:, 1:2], -1.0, 1.0, ALU.mult, ALU.add).then_inc(s_leak, 1)
                dve.wait_ge(s_leak, 1)

                def step(i, r, scan_on, proj_on, rel_on):
                    m = i * 2 + r
                    if proj_on and not scan_on:
                        for g in range(VG):
                            dve.wait_ge(s_vps, g + 1)
                            if g >= 2:
                                dve.wait_ge(s_vp, g - 1)
                            dve.tensor_tensor(vf[g % 2][:].rearrange("p (b h) d -> p b (h d)", b=4),
                                              ps[g % 2][:].rearrange("p (b e) -> p b e", b=4),
                                              bv_bc[:].unsqueeze(1).broadcast_to([P, 4, D]), ALU.add).then_inc(s_vf, 1)
                    for j in range(TC):
                        if scan_on:
                            t = m * TC + j
                            dve.wait_ge(s_gate, t + 1)
                            dve.tensor_tensor(upd[:].unsqueeze(1), gate[:].unsqueeze(1), xT[:, bass.ds(t, 1), :],
                                              ALU.mult).then_inc(s_upd, 1)
                            dve.wait_ge(s_upd, t + 1)
                            dve.scalar_tensor_tensor(out=pre[:].unsqueeze(1), in0=hs[:, bass.ds(t, 1), :],
                                                     scalar=leak[:, 0:1], in1=upd[:].unsqueeze(1),
                                                     op0=ALU.mult, op1=ALU.add).then_inc(s_pre, 1)
                        if rel_on:
                            c = m - 2
                            dve.wait_ge(s_s2, c * TC + j + 2)
                            if j % 4 == 0:
                                dve.wait_ge(s_s2w[j // 4], c * 16 + 16)
                            dve.tensor_copy(stage[j // 4][:, :, j % 4, :],
                                            ps[4 + j % 4][:].rearrange("p (g k) -> p g k", k=T)).then_inc(s_s2c, 1)

                macros(dve, step)

            @block.gpsimd
            def _(pool):
                pool.sem_inc(s_qp, 1)
                pool.sem_inc(s_kp, 1)

                def split(parts, rest, link, last):
                    link(pool.tensor_copy(parts[0], rest))
                    link(pool.tensor_tensor(rest, rest, parts[0], ALU.subtract))
                    link(pool.tensor_copy(parts[1], rest))
                    last(pool.tensor_tensor(parts[2], rest, parts[1], ALU.subtract))

                n_rel = [0]

                def rel_link(op):
                    n_rel[0] += 1
                    op.then_inc(s_rel, 1)
                    pool.wait_ge(s_rel, n_rel[0])

                pool.wait_ge(s_rel_in, 32)
                split([rkp[:, n, :] for n in range(NP)], rk[:], rel_link, lambda op: op.then_inc(s_rkp, 1))
                for t9 in (V27[:].rearrange("p b h n d -> p (b h) n d"), relv27[:]):
                    pool.memset(t9[:, :, 0, DH:], 1.0)
                    rel_link(pool.memset(t9[:, :, 1:, DH:], 0.0))
                split([relv27[:, :, n, 0:DH] for n in range(NP)], relv[:], rel_link, rel_link)

                def step(i, r, scan_on, proj_on, rel_on):
                    if not proj_on:
                        return
                    m = i * 2 + r
                    o = 1 - r
                    fill = i if r else i - 1
                    ts = bass.ds((m - 1) * TC, TC)
                    n = [0]

                    def link(op):
                        n[0] += 1
                        op.then_inc(s_pc, 1)
                        pool.wait_ge(s_pc, (m - 1) * PLINKS + n[0])
                        pool.sem_inc(s_pass, 1)

                    pool.wait_ge(s_qf, m + 1)
                    pool.wait_ge(s_qw[o], fill * (16 * NP) + 16)
                    pool.sem_inc(s_pass, 1)
                    split([qp[o][:, x, :] for x in range(NP)], qf[:].rearrange("p b t -> p (b t)"), link,
                          lambda op: op.then_inc(s_qp, 1))
                    pool.wait_ge(s_qp, m + 1)
                    pool.sem_inc(s_pass, 1)
                    link(pool.tensor_copy(qfull[:, :, :, ts], qp[o][:].rearrange("p i (b t) -> p i b t", t=TC)))
                    pool.wait_ge(s_kf, m + 1)
                    pool.sem_inc(s_pass, 1)
                    split([kfull[:, x, :, ts] for x in range(NP)], kf[:], link, lambda op: op.then_inc(s_kp, 1))
                    assert n[0] == PLINKS
                    if not scan_on:
                        nv = [0]

                        def vlink(op):
                            nv[0] += 1
                            op.then_inc(s_vc, 1)
                            pool.wait_ge(s_vc, nv[0])

                        for g in range(VG):
                            pool.wait_ge(s_vf, g + 1)
                            v = V27[:, 4 * g:4 * g + 4].rearrange("p b h n d -> p (b h) n d")
                            split([v[:, :, x, 0:DH] for x in range(NP)], vf[g % 2][:], vlink,
                                  lambda op: op.then_inc(s_vp, 1))

                macros(pool, step)
        scan.close()

        with ExitStack() as st4:
            def sb4(name, shape, dt=F32):
                return st4.enter_context(nc.sbuf_tensor(name, shape, dt))

            HH = H // 2
            NU = 2 * GB
            RING = 4
            LAG = 3
            PAIRS = GB // 2
            PSCALE = 1024.0
            PTh = sb4("PTh", [P, P, T], F16)
            PTl = sb4("PTl", [P, P, T], F16)
            QS = [sb4(f"QS{i}", [KS, H, 2 * T], BF16) for i in range(2)]
            KSt = [sb4(f"KS{i}", [KS, H, 2 * T], BF16) for i in range(2)]
            s2t = [sb4(f"s2t{i}", [P, HH, T]) for i in range(RING)]
            sc = [sb4(f"sc{i}", [P, HH, T]) for i in range(RING)]
            mx = [sb4(f"mx{i}", [P, HH]) for i in range(RING)]
            w1s = [sb4(f"w1s{i}", [P, H, DH + 1]) for i in range(2)]
            w1n = [sb4(f"w1n{i}", [P, H, DH]) for i in range(2)]
            rc1 = [sb4(f"rc1_{i}", [P, H]) for i in range(2)]
            QC = 16
            NQC = T // QC
            w2a = [sb4(f"w2a{i}", [P, QC, DH + 1]) for i in range(2)]
            w2n = [sb4(f"w2n{i}", [P, QC, DH]) for i in range(2)]
            w2s = [sb4(f"w2s{i}", [P, P]) for i in range(2)]
            rc2 = [sb4(f"rc2_{i}", [P, QC]) for i in range(2)]

            s_qks = [sem(f"operand_stacks_loaded{i}") for i in range(2)]
            s_s1 = sem("content_scores_ready")
            s_s2l = [sem(f"relative_scores_loaded{i}") for i in range(RING)]
            s_add = sem("scores_summed")
            s_max = sem("row_maxima_ready")
            s_sub = sem("maxima_subtracted")
            s_exp = sem("exp_ready")
            s_tr = sem("exp_transposed")
            s_pth = sem("first_parts_ready")
            s_ptl = sem("second_parts_ready")
            s_w1 = sem("value_product_ready")
            s_v1 = sem("value_product_chain")
            s_w1n = sem("value_product_normalised")
            s_w1t = sem("value_product_transposed")
            s_w1c = sem("value_product_stored")
            s_w2 = sem("relative_value_product_ready")
            s_v2 = sem("relative_value_product_chain")
            s_w2n = sem("relative_value_product_normalised")
            s_w2t = sem("relative_value_product_transposed")
            s_w2c = sem("relative_value_product_copied")
            s_w2d = [sem(f"relative_value_product_written{i}") for i in range(2)]
            s2_in = s2_dram.rearrange("(h p r) q k -> q h p r k", h=H, r=2)

            with nc.Block() as block:
                @block.sync
                def _(sp):
                    def load_stacks(g, p):
                        at = bass.ds((g * PAIRS + p) * (2 * T), 2 * T)
                        for tile, dram in ((QS[p % 2], qbt_dram), (KSt[p % 2], kbt_dram)):
                            sp.dma_start(tile[:], dram[:, :, :, at].rearrange("j i (d h) x -> (j i d) h x", h=H))\
                              .then_inc(s_qks[p % 2], 16)

                    with sp.Fori(0, 2) as gp:
                        with sp.Fori(0, 2) as gm:
                            g = gp * 2 + gm
                            sp.wait_ge(s_s1, g * NU + 1)
                            sp.sem_inc(s_spass, 1)
                            load_stacks(g, 0)
                            load_stacks(g, 1)
                            for u in range(NU):
                                sp.wait_ge(s_add, g * NU + max(u - RING + 1, 0) + 1)
                                sp.sem_inc(s_spass, 1)
                                half = u % 2
                                src = s2_in[:, bass.ds(gm * GB + u // 2, 1), half * HH:(half + 1) * HH,
                                            bass.ds(gp, 1), :]
                                sp.dma_start(s2t[u % RING][:], src.rearrange("q a p r k -> q (a p r) k"))\
                                  .then_inc(s_s2l[u % RING], 16)
                                if u % 4 == 3 and 7 <= u < 15:
                                    load_stacks(g, (u - 7) // 4 + 2)

                @block.gpsimd
                def _(pool):
                    with pool.Fori(0, NG) as g:
                        for u in range(NU):
                            pool.wait_ge(s_max, g * NU + u + 1)
                            pool.tensor_tensor(sc[u % RING][:], sc[u % RING][:],
                                               mx[u % RING][:].unsqueeze(2).broadcast_to([P, HH, T]), ALU.subtract)\
                                .then_inc(s_sub, 1)

                @block.tensor
                def _(pe):
                    pe.sem_inc(s_s1, 1)
                    pe.sem_inc(s_w2, 1)

                    def w1_turn(g, bl):
                        pe.wait_ge(s_w1n, g * GB + bl + 2)
                        if bl == 0:
                            pe.wait_ge(s_w2n, g * NQC + 1)
                        pe.wait_ge(s_w1c, g * GB + bl + 1)
                        pe.transpose(ps[7][:, 0:T], w1n[bl % 2][:].rearrange("p h d -> p (h d)"), ident[:])\
                          .then_inc(s_w1t, 1)

                    with pe.Fori(0, NG) as g:
                        for u in range(NU + 5):
                            if u < NU:
                                bl, half = u // 2, u % 2
                                if u % 4 == 0:
                                    p = bl // 2
                                    pe.wait_ge(s_qks[p % 2], (g * (PAIRS // 2) + p // 2 + 1) * 32)
                                if u >= 2:
                                    pe.wait_ge(s_add, g * NU + u)
                                for h in range(HH):
                                    x = slice(bl % 2 * T, (bl % 2 + 1) * T)
                                    mm = pe.matmul(ps[2 * (u % 2) + h // 4][:, h % 4 * T:(h % 4 + 1) * T],
                                                   QS[bl // 2 % 2][:, half * HH + h, x],
                                                   KSt[bl // 2 % 2][:, half * HH + h, x], start=True, stop=True)
                                mm.then_inc(s_s1, 1)
                            if u >= 5 and u % 2:
                                bl = (u - 5) // 2
                                pe.wait_ge(s_ptl, (g * NU + 2 * bl + 2) * 2 + 1)
                                pe.wait_ge(s_w1n, g * GB + bl + 1)
                                for h in range(H):
                                    for part in (PTh, PTl):
                                        mm = pe.matmul(ps[6][:, h * VW:(h + 1) * VW], part[:, bl * H + h, :],
                                                       V27[:, bass.ds(g * GB + bl, 1), h].rearrange(
                                                           "p b n d -> p (b n d)"),
                                                       start=(part is PTh), stop=(part is PTl))
                                mm.then_inc(s_w1, 1)
                            if LAG <= u < NU + LAG:
                                v = u - LAG
                                pe.wait_ge(s_exp, g * NU + v + 1)
                                if v == 0:
                                    pe.wait_ge(s_w2c, g * NQC + 1)
                                for s in range(2):
                                    if v:
                                        pe.wait_ge(s_ptl, (g * NU + v) * 2 + s)
                                    for j in range(4):
                                        mm = pe.transpose(ps[4 + s][:, j * T:(j + 1) * T],
                                                          sc[v % RING][:, 4 * s + j, :], ident[:])
                                    mm.then_inc(s_tr, 1)
                            if u >= 6 and u % 2 == 0:
                                w1_turn(g, (u - 6) // 2)
                        for c in range(NQC + 1):
                            if c < NQC:
                                if c == 0:
                                    pe.wait_ge(s_w1c, g * GB + GB + 1)
                                elif c >= 2:
                                    pe.wait_ge(s_w2n, g * NQC + c)
                                for j in range(QC):
                                    q = QC * c + j
                                    for part in (PTh, PTl):
                                        mm = pe.matmul(ps[7 - c % 2][:, j * VW:(j + 1) * VW], part[:, :, q],
                                                       relv27[:, T - 1 - q].rearrange("p n d -> p (n d)"),
                                                       start=(part is PTh), stop=(part is PTl))
                                mm.then_inc(s_w2, 1)
                            if c >= 1:
                                n = c - 1
                                pe.wait_ge(s_w2n, g * NQC + c + 1)
                                if n >= 2:
                                    pe.wait_ge(s_w2c, g * NQC + n)
                                pe.transpose(ps[4 + n % 2][:, 0:P], w2n[n % 2][:].rearrange("p q d -> p (q d)"),
                                             ident[:]).then_inc(s_w2t, 1)

                @block.vector
                def _(dve):
                    dve.sem_inc(s_add, 1)
                    dve.sem_inc(s_w1n, 1)
                    dve.sem_inc(s_ptl, 1)
                    dve.sem_inc(s_w2n, 1)

                    def normalise(s_chain, links, bank, n, summed, rec, out, ready):
                        parts = ps[bank][:, 0:n * VW].rearrange("p (n x d) -> p n d x", x=NP, d=DH + 1)
                        dve.tensor_reduce(summed[:], parts, AX.X, ALU.add).then_inc(s_chain, 1)
                        dve.wait_ge(s_chain, links + 1)
                        dve.reciprocal(rec[:].unsqueeze(2), summed[:, :, DH:]).then_inc(s_chain, 1)
                        dve.wait_ge(s_chain, links + 2)
                        dve.tensor_tensor(out[:], summed[:, :, 0:DH], rec[:].unsqueeze(2).broadcast_to([P, n, DH]),
                                          ALU.mult).then_inc(ready, 1)

                    with dve.Fori(0, NG) as g:
                        for u in range(NU + 5):
                            if u < NU:
                                r = u % RING
                                dve.wait_ge(s_s1, g * NU + u + 2)
                                dve.wait_ge(s_s2l[r], (g * (NU // RING) + u // RING + 1) * 16)
                                if u >= RING:
                                    dve.wait_ge(s_tr, (g * NU + u - RING + 1) * 2)
                                for s in range(2):
                                    op = dve.tensor_tensor(sc[r][:, 4 * s:4 * s + 4, :],
                                                           ps[2 * (u % 2) + s][:].rearrange("p (h k) -> p h k", k=T),
                                                           s2t[r][:, 4 * s:4 * s + 4, :], ALU.add)
                                op.then_inc(s_add, 1)
                                dve.wait_ge(s_add, g * NU + u + 2)
                                dve.tensor_reduce(mx[r][:], sc[r][:], AX.X, ALU.max).then_inc(s_max, 1)
                            if LAG <= u < NU + LAG:
                                v = u - LAG
                                for s in range(2):
                                    rows = slice(v * HH + 4 * s, v * HH + 4 * s + 4)
                                    dve.wait_ge(s_pth, (g * NU + v) * 2 + s + 1)
                                    dve.scalar_tensor_tensor(out=PTl[:, rows, :].rearrange("p h q -> p (h q)"),
                                                             in0=ps[4 + s][:], scalar=PSCALE,
                                                             in1=PTh[:, rows, :].rearrange("p h q -> p (h q)"),
                                                             op0=ALU.mult, op1=ALU.subtract).then_inc(s_ptl, 1)
                            if u >= 5 and u % 2:
                                bl = (u - 5) // 2
                                dve.wait_ge(s_w1, g * GB + bl + 1)
                                if bl >= 2:
                                    dve.wait_ge(s_w1t, g * GB + bl - 1)
                                normalise(s_v1, (g * GB + bl) * 2, 6, H, w1s[bl % 2], rc1[bl % 2], w1n[bl % 2], s_w1n)
                        for c in range(NQC):
                            dve.wait_ge(s_w2, g * NQC + c + 2)
                            if c >= 2:
                                dve.wait_ge(s_w2t, g * NQC + c - 1)
                            normalise(s_v2, (g * NQC + c) * 2, 7 - c % 2, QC, w2a[c % 2], rc2[c % 2], w2n[c % 2], s_w2n)

                @block.scalar
                def _(act):
                    act.sem_inc(s_w2c, 1)
                    act.sem_inc(s_w1c, 1)
                    for r in range(2):
                        act.sem_inc(s_w2d[r], 16)
                    act.preload_act_table_set("exp_and_others")
                    with act.Fori(0, NG) as g:
                        for u in range(NU + 5):
                            if u < NU:
                                act.wait_ge(s_sub, g * NU + u + 1)
                                act.activation(sc[u % RING][:], sc[u % RING][:], ACT.Exp, scale=DH ** -0.5)\
                                   .then_inc(s_exp, 1)
                            if LAG <= u < NU + LAG:
                                v = u - LAG
                                for s in range(2):
                                    act.wait_ge(s_tr, (g * NU + v) * 2 + s + 1)
                                    if v == 0 and s == 0:
                                        act.wait_ge(s_w2, g * NQC + 1)
                                    act.activation(PTh[:, v * HH + 4 * s:v * HH + 4 * s + 4, :],
                                                   ps[4 + s][:].rearrange("p (h q) -> p h q", q=T), ACT.Copy,
                                                   scale=PSCALE).then_inc(s_pth, 1)
                            if u >= 6 and u % 2 == 0:
                                bl = (u - 6) // 2
                                act.wait_ge(s_w1t, g * GB + bl + 1)
                                act.activation(OT1[:, bass.ds(g * GB + bl, 1), :], ps[7][:, 0:T].unsqueeze(1), ACT.Copy)\
                                   .then_inc(s_w1c, 1)
                        for n in range(NQC):
                            act.wait_ge(s_w2t, g * NQC + n + 1)
                            act.wait_ge(s_w2d[n % 2], (g * (NQC // 2) + n // 2) * 16 + 16)
                            act.activation(w2s[n % 2][:], ps[4 + n % 2][:, 0:P], ACT.Copy).then_inc(s_w2c, 1)
                            act.wait_ge(s_w2c, g * NQC + n + 2)
                            act.dma_start(w2_dram[n * P:(n + 1) * P, bass.ds(g * P, P)], w2s[n % 2][:])\
                               .then_inc(s_w2d[n % 2], 16)
                    for r in range(2):
                        act.wait_ge(s_w2d[r], 16 * NG * (NQC // 2) + 16)
        att.close()

        with ExitStack() as st5:
            OT2 = st5.enter_context(nc.sbuf_tensor("OT2", [P, T, B], F32))
            s_ot2 = sem("relative_value_outputs_loaded")
            s_y = sem("output_projection_ready")
            s_x1 = sem("residual_ready")
            with nc.Block() as block:
                w2_in = w2_dram.rearrange("(q d) (h b) -> h d q b", d=DH, b=B)

                @block.sync
                def _(sp):
                    for h in range(0, H, 2):
                        sp.dma_start(OT2[h * DH:(h + 1) * DH, :, :], w2_in[h]).then_inc(s_ot2, 16)

                @block.scalar
                def _(act):
                    for h in range(1, H, 2):
                        act.dma_start(OT2[h * DH:(h + 1) * DH, :, :], w2_in[h]).then_inc(s_ot2, 16)

                @block.tensor
                def _(pe):
                    pe.wait_ge(s_ot2, 16 * H)
                    for c in range(NCH):
                        ts = slice(c * TC, (c + 1) * TC)
                        if c >= 2:
                            pe.wait_ge(s_x1, c - 1)
                        pe.matmul(ps[c % 2][:], wo[:], OT1[:, :, ts].rearrange("p b t -> p t b"), start=True, stop=False)
                        pe.matmul(ps[c % 2][:], wo[:], OT2[:, ts, :], start=False, stop=True).then_inc(s_y, 1)

                @block.vector
                def _(dve):
                    for c in range(NCH):
                        ts = slice(c * TC, (c + 1) * TC)
                        dve.wait_ge(s_y, c + 1)
                        dve.scalar_tensor_tensor(out=xT[:, ts, :].rearrange("p t b -> p (t b)"), in0=ps[c % 2][:],
                                                 scalar=cols[:, 4:5], in1=xT[:, ts, :].rearrange("p t b -> p (t b)"),
                                                 op0=ALU.add, op1=ALU.add).then_inc(s_x1, 1)

        h2 = sb("h2", [P, T + 1, B])
        w1T = sb("w1T", [P, E, FF])
        w2T = sb("w2T", [P, E, FC, D])
        b1c = sb("b1c", [P, E, FC])
        b2r = sb("b2r", [E, D])
        rwT = sb("rwT", [P, E])
        iota = sb("iota", [P, E])
        s_c2 = sem("scan2_state_loaded")
        s_ffn_in = sem("ffn_inputs_loaded")
        s_r = sem("scan2_sums_ready")
        s_h2 = sem("scan2_state_ready")
        with nc.Block() as block:
            @block.sync
            def _(sp):
                sp.dma_start(h2[:, 0, :], a["condT"]).then_inc(s_c2, 16)
                for dst, src in ((w1T[:], a["w1T"]), (w2T[:], a["w2T"]), (b1c[:], a["b1c"]), (b2r[:], a["b2"]),
                                 (rwT[:], a["rwT"]), (iota[:], a["iota"].partition_broadcast(P))):
                    sp.dma_start(dst, src).then_inc(s_ffn_in, 16)

            @block.tensor
            def _(pe):
                pe.wait_ge(s_c2, 16)
                with pe.Fori(0, T // 2) as i:
                    for r in range(2):
                        t = i * 2 + r
                        pe.matmul(ps[r][:, 0:B], wx2[:], xT[:, bass.ds(t, 1), :], start=True, stop=False)
                        pe.wait_ge(s_h2, t + 1)
                        pe.matmul(ps[r][:, 0:B], wh2[:], h2[:, bass.ds(t, 1), :], start=False, stop=True)\
                          .then_inc(s_r, 1)

            @block.scalar
            def _(act):
                act.sem_inc(s_h2, 1)
                act.wait_ge(s_c2, 16)
                with act.Fori(0, T // 2) as i:
                    for r in range(2):
                        t = i * 2 + r
                        act.wait_ge(s_r, t + 1)
                        act.activation(h2[:, bass.ds(t + 1, 1), :], ps[r][:, 0:B].unsqueeze(1), ACT.Tanh,
                                       bias=cols[:, 5:6]).then_inc(s_h2, 1)

        xc = [sb(f"xc{i}", [P, BANK]) for i in range(2)]
        rc = [sb(f"resc{i}", [P, BANK]) for i in range(2)]
        hid = [sb(f"hid{i}", [P, FC, BANK]) for i in range(2)]
        top = sb("top", [P, JT, 8])
        topi = sb("topi", [P, JT, 8], U32)
        topf = sb("topf", [P, JT, 8])
        lg = sb("lg", [P, JT, E])
        lgc = sb("lgc", [P, JT, E])
        ex = sb("ex", [P, JT, E])
        small = sb("small", [P, 4, JT])
        w01 = sb("w01", [P, JT, 2])
        sel = sb("sel", [P, 2, JT, E])
        cw = sb("cw", [P, JT, E])
        cwT = sb("cwT", [E, JT, P])
        acc = [sb(f"acc{i}", [P, JT, D]) for i in range(2)]
        s_xc = sem("chunk_operands_ready")
        s_lg = sem("logits_ready")
        s_v = sem("vector_chain")
        s_ea = sem("router_shift_ready")
        s_eb = sem("router_exp_ready")
        s_cw = sem("combine_weights_ready")
        s_cwt = sem("combine_weights_transposed")
        s_cwc = sem("combine_weights_copied")
        s_b2 = sem("start_rows_ready")
        s_acc0 = sem("start_rows_copied")
        s_up = sem("hidden_sums_ready")
        s_hid = sem("hidden_ready")
        s_dn = sem("expert_rows_ready")
        s_mix = sem("expert_rows_added")
        s_out = [sem(f"output_written{i}") for i in range(2)]
        with nc.Block() as block:
            @block.gpsimd
            def _(pool):
                def operands(c, r):
                    pool.tensor_copy(xc[r][:].rearrange("p (t b) -> p t b", b=B), h2[:, bass.ds(c * TC + 1, TC), :])
                    pool.tensor_copy(rc[r][:].rearrange("p (t b) -> p t b", b=B), xT[:, bass.ds(c * TC, TC), :])\
                        .then_inc(s_xc, 1)

                operands(0, 0)
                operands(1, 1)
                with pool.Fori(1, NCH // 2) as i:
                    for r in range(2):
                        pool.wait_ge(s_mix, (i * 2 + (r - 1)) * E + 1)
                        operands(i * 2 + r, r)

            @block.tensor
            def _(pe):
                pe.sem_inc(s_dn, 1)
                pe.wait_ge(s_ffn_in, 16 * 6)
                with pe.Fori(0, NCH // 2) as i:
                    for r in range(2):
                        c = i * 2 + r
                        pe.wait_ge(s_xc, c + 1)
                        pe.wait_ge(s_cwc, c + 1)
                        for j in range(JT):
                            mm = pe.matmul(ps[6][:, j * E:(j + 1) * E], xc[r][:, j * P:(j + 1) * P], rwT[:],
                                           start=True, stop=True)
                        mm.then_inc(s_lg, 1)

                        def up(e):
                            for f in range(FC):
                                pe.wait_ge(s_hid, (c * E + e) * FC - (FC - 1 - f if e else 0) + 1)
                                pe.matmul(ps[f][:], w1T[:, e, f * P:(f + 1) * P], xc[r][:], start=True, stop=True)\
                                  .then_inc(s_up, 1)

                        def start_rows():
                            pe.wait_ge(s_cw, c + 1)
                            for j in range(JT):
                                mm = pe.transpose(ps[6][0:E, j * P:(j + 1) * P], cw[:, j, :], ident[:])
                            mm.then_inc(s_cwt, 1)
                            pe.wait_ge(s_cwc, c + 2)
                            pe.wait_ge(s_acc0, c + 1)
                            for j in range(JT):
                                pe.matmul(ps[7][:, j * D:(j + 1) * D], rc[r][:, j * P:(j + 1) * P], ident[:],
                                          start=True, stop=False)
                                mm = pe.matmul(ps[7][:, j * D:(j + 1) * D], cwT[:, j, :], b2r[:],
                                               start=False, stop=True)
                            mm.then_inc(s_b2, 1)

                        def down(e):
                            n = c * E + e
                            pe.wait_ge(s_hid, (n + 1) * FC + 1)
                            pe.wait_ge(s_mix, n - min(e, 1) + 1)
                            for j in range(JT):
                                for f in range(FC):
                                    mm = pe.matmul(ps[4 + e % 2][:, j * D:(j + 1) * D],
                                                   hid[e % 2][:, f, j * P:(j + 1) * P], w2T[:, e, f, :],
                                                   start=(f == 0), stop=(f == FC - 1))
                            mm.then_inc(s_dn, 1)

                        up(0)
                        for e in range(E):
                            if e + 1 < E:
                                up(e + 1)
                            if e == 0:
                                start_rows()
                            down(e)

            @block.scalar
            def _(act):
                act.sem_inc(s_hid, 1)
                act.wait_ge(s_ffn_in, 16 * 6)
                with act.Fori(0, NCH) as c:
                    act.wait_ge(s_ea, c + 1)
                    act.activation(ex[:], lg[:], ACT.Exp).then_inc(s_eb, 1)
                    for e in range(E):
                        n = c * E + e
                        act.wait_ge(s_dn, n - min(e, 1) + 1)
                        for f in range(FC):
                            act.wait_ge(s_up, n * FC + f + 1)
                            act.activation(hid[e % 2][:, f, :], ps[f][:], ACT.Gelu, bias=b1c[:, e, f:f + 1])\
                               .then_inc(s_hid, 1)

            @block.vector
            def _(dve):
                dve.sem_inc(s_cwc, 1)
                dve.sem_inc(s_acc0, 1)
                dve.sem_inc(s_mix, 1)
                dve.wait_ge(s_ffn_in, 16 * 6)
                STEPS = 10
                with dve.Fori(0, NCH // 2) as i:
                    for r in range(2):
                        c = i * 2 + r
                        base = c * STEPS
                        k = [0]

                        def link(op):
                            k[0] += 1
                            op.then_inc(s_v, 1)
                            dve.wait_ge(s_v, base + k[0])

                        dve.wait_ge(s_lg, c + 1)
                        logits = ps[6][:, 0:JT * E].rearrange("p (j e) -> p j e", e=E)
                        link(dve.tensor_copy(lgc[:], logits))
                        dve.tensor_reduce(small[:, 0, :], lgc[:], AX.X, ALU.max)
                        for j in range(JT):
                            op = dve.max(top[:, j, :], lgc[:, j, :])
                        link(op)
                        dve.tensor_tensor(lg[:], lgc[:], small[:, 0, :].unsqueeze(2).broadcast_to([P, JT, E]),
                                          ALU.subtract).then_inc(s_ea, 1)
                        for j in range(JT):
                            op = dve.max_index(topi[:, j, :], top[:, j, :], lgc[:, j, :])
                        link(op)
                        link(dve.tensor_copy(topf[:], topi[:]))
                        dve.wait_ge(s_eb, c + 1)
                        dve.tensor_reduce(small[:, 0, :], ex[:], AX.X, ALU.add)
                        for x in range(2):
                            op = dve.tensor_tensor(sel[:, x], iota[:].unsqueeze(1).broadcast_to([P, JT, E]),
                                                   topf[:, :, x:x + 1].broadcast_to([P, JT, E]), ALU.is_equal)
                        link(op)
                        link(dve.tensor_tensor(cw[:], sel[:, 0], sel[:, 1], ALU.add))
                        link(dve.tensor_tensor(cw[:], cw[:], ex[:], ALU.mult))
                        link(dve.tensor_reduce(small[:, 1, :], cw[:], AX.X, ALU.add))
                        link(dve.scalar_tensor_tensor(out=small[:, 2, :], in0=small[:, 0, :], scalar=1e-9,
                                                      in1=small[:, 1, :], op0=ALU.mult, op1=ALU.add))
                        link(dve.reciprocal(small[:, 3, :], small[:, 2, :]))
                        dve.tensor_tensor(cw[:], cw[:], small[:, 3, :].unsqueeze(2).broadcast_to([P, JT, E]),
                                          ALU.mult).then_inc(s_cw, 1)
                        dve.wait_ge(s_cw, c + 1)
                        dve.wait_ge(s_cwt, c + 1)
                        dve.tensor_copy(cwT[:].rearrange("p j t -> p (j t)"), ps[6][0:E, :]).then_inc(s_cwc, 1)
                        dve.wait_ge(s_b2, c + 1)
                        dve.wait_ge(s_out[r], i * 16 + 16)
                        dve.tensor_copy(acc[r][:].rearrange("p j d -> p (j d)"), ps[7][:]).then_inc(s_acc0, 1)
                        dve.wait_ge(s_acc0, c + 2)
                        for e in range(E):
                            dve.wait_ge(s_dn, c * E + e + 2)
                            if e >= 1:
                                dve.wait_ge(s_mix, c * E + e + 1)
                            for j in range(JT):
                                op = dve.scalar_tensor_tensor(out=acc[r][:, j, :],
                                                              in0=ps[4 + e % 2][:, j * D:(j + 1) * D],
                                                              scalar=cw[:, j, e:e + 1], in1=acc[r][:, j, :],
                                                              op0=ALU.mult, op1=ALU.add)
                            op.then_inc(s_mix, 1)
                        assert k[0] == STEPS

            @block.sync
            def _(sp):
                sp.sem_inc(s_out[0], 16)
                sp.sem_inc(s_out[1], 16)
                with sp.Fori(0, NCH // 2) as i:
                    for r in range(2):
                        c = i * 2 + r
                        sp.wait_ge(s_mix, (c + 1) * E + 1)
                        sp.dma_start(a["out"].rearrange("(c j p) d -> c p j d", j=JT, p=P)[bass.ds(c, 1)]
                                     .rearrange("c p j d -> (c p) j d"), acc[r][:]).then_inc(s_out[r], 16)
                for r in range(2):
                    sp.wait_ge(s_out[r], 16 * (NCH // 2) + 16)


def kernel(x, cond_1024, L0_cond_W, L0_cond_b, L0_cond_alpha, L0_attn_Wq, L0_attn_bq, L0_attn_Wk, L0_attn_bk,
           L0_attn_Wv, L0_attn_bv, L0_attn_Wo, L0_attn_bo, L0_attn_rel_k_emb, L0_attn_rel_v_emb,
           L0_cond2_Wx, L0_cond2_Wh, L0_cond2_b, L0_ffn_router_w, L0_ffn_expert_w1, L0_ffn_expert_b1,
           L0_ffn_expert_w2, L0_ffn_expert_b2):
    import numpy as np
    import concourse.bacc as bacc
    from concourse.bass_utils import run_bass_kernel_spmd

    f = np.asarray
    dh = np.arange(P).reshape(H, DH).T.ravel()
    arrays = {
        "xT": f(x).transpose(2, 1, 0),
        "condT": f(cond_1024).T,
        "wh": f(L0_cond_W)[:, :D].T, "wz": f(L0_cond_W)[:, D:].T,
        "wq": f(L0_attn_Wq)[dh].T, "wk": f(L0_attn_Wk)[dh].T, "wv": f(L0_attn_Wv).T, "wo": f(L0_attn_Wo).T,
        "wx2": f(L0_cond2_Wx), "wh2": f(L0_cond2_Wh),
        "cols": np.stack([f(v) for v in (L0_cond_b, L0_cond_alpha, f(L0_attn_bq)[dh], f(L0_attn_bk)[dh], L0_attn_bo,
                                         L0_cond2_b)], axis=1),
        "bv": f(L0_attn_bv),
        "relk": f(L0_attn_rel_k_emb)[REL:0:-1].T,
        "relv": f(L0_attn_rel_v_emb)[REL:0:-1],
        "ident": np.eye(P, dtype=np.float32),
        "w1T": f(L0_ffn_expert_w1).transpose(2, 0, 1),
        "w2T": f(L0_ffn_expert_w2).reshape(E, D, FC, P).transpose(3, 0, 2, 1),
        "b1c": f(L0_ffn_expert_b1).reshape(E, FC, P).transpose(2, 0, 1),
        "b2": f(L0_ffn_expert_b2),
        "rwT": f(L0_ffn_router_w).T,
        "iota": np.arange(E, dtype=np.float32),
    }
    arrays = {n: np.ascontiguousarray(v) for n, v in arrays.items()}
    nc = bacc.Bacc("TRN2", target_bir_lowering=False, num_devices=1)
    a = {n: nc.dram_tensor(f"in_{n}", v.shape, mybir.dt.from_np(v.dtype), kind="ExternalInput").ap()
         for n, v in arrays.items()}
    a["out"] = nc.dram_tensor("out_rows", (T * B, D), F32, kind="ExternalOutput").ap()
    build(nc, a)
    r = run_bass_kernel_spmd(nc, [{f"in_{n}": v for n, v in arrays.items()}], core_ids=[0])
    return r.results[0]["out_rows"].reshape(T, B, D).transpose(1, 0, 2)
```

```python
from contextlib import ExitStack

import concourse.bass as bass
from concourse import mybir

F32 = mybir.dt.float32
BF16 = mybir.dt.bfloat16
F16 = mybir.dt.float16
U32 = mybir.dt.uint32
I32 = mybir.dt.int32
ALU = mybir.AluOpType
ACT = mybir.ActivationFunctionType
AX = mybir.AxisListType

P = 128
B = 32
T = 128
D = 128
H = 16
DH = D // H
QUAD = 4
NHG = H // QUAD
BANK = 512
E = 8
FF = 512
FC = FF // P
TC = BANK // B
NCH = T // TC
JT = BANK // P
GB = 8
NG = B // GB
N = B * T
NT = N // P
CAP = N + P
NS = 72
NULL = NS - 2 * N // P
MT = NT + 1
REL = 2 * T - 1
NP = 3
KS = NP * NP * DH


def build(nc, a):
    with ExitStack() as ctx:
        def sb(name, shape, dt=F32):
            return ctx.enter_context(nc.sbuf_tensor(name, shape, dt))

        def sem(name):
            return ctx.enter_context(nc.semaphore(name))

        s2_dram = nc.dram_tensor("s2_scratch", (H * B, T, T), F32).ap()
        w2_dram = nc.dram_tensor("w2_scratch", (T * DH, H * B), F32).ap()
        qtb_dram = nc.dram_tensor("qtb_scratch", (NCH, NP, DH * H, BANK), BF16).ap()
        qbt_dram = nc.dram_tensor("qbt_scratch", (NP, DH * H, B * T), BF16).ap()
        kbt_dram = nc.dram_tensor("kbt_scratch", (NP, DH * H, B * T), BF16).ap()
        rk_dram = nc.dram_tensor("rk_scratch", (NP, NP, DH, REL), BF16).ap()

        ident = sb("ident", [P, P])
        xT = sb("xT", [P, T, B])
        wz, wh = sb("wz", [P, D]), sb("wh", [P, D])
        wq, wk, wv, wo = (sb(n, [P, D]) for n in ("wq", "wk", "wv", "wo"))
        wx2, wh2 = sb("wx2", [P, D]), sb("wh2", [P, D])
        cols = sb("cols", [P, 6])
        bv_bc = sb("bv_bc", [P, D])
        leak = sb("leak", [P, 1])
        hs = sb("hs", [P, T, B])
        OT1 = hs[:].rearrange("p t b -> p (t b)").rearrange("p (b t) -> p b t", t=T)
        att = ctx.enter_context(ExitStack())

        def sba(name, shape, dt=F32):
            return att.enter_context(nc.sbuf_tensor(name, shape, dt))

        VW = NP * (DH + 1)
        V27 = sba("V27", [P, B, H, NP, DH + 1], BF16)
        relv27 = sba("relv27", [P, T, NP, DH + 1], BF16)
        scan = ctx.enter_context(ExitStack())

        def sbs(name, shape, dt=F32):
            return scan.enter_context(nc.sbuf_tensor(name, shape, dt))

        x0 = sbs("x0", [P, TC, B, 2])
        h1 = [sbs(f"h1_{i}", [P, TC, B]) for i in range(2)]
        gl = sbs("gl", [P, B, 2])
        pre = sbs("pre", [P, B, 2])
        rkp = sbs("rkp", [DH, NP, REL], BF16)
        relkS = sbs("relkS", [KS, REL], BF16)
        relv = sbs("relv", [P, T, DH])
        qf = sbs("qf", [P, B, TC])
        kf = sbs("kf", [P, B, TC])
        qp = [sbs(f"qp{i}", [P, NP, BANK], BF16) for i in range(2)]
        qfull = sbs("qfull", [P, NP, B, T], BF16)
        kfull = sbs("kfull", [P, NP, B, T], BF16)
        QS2 = [sbs(f"QS2_{i}", [KS, H, BANK], BF16) for i in range(2)]
        SETS = TC // 4
        stage = [sbs(f"s2stage{i}", [P, NHG, 4, T]) for i in range(SETS)]
        rk = stage[0][0:DH].rearrange("p g q k -> p (g q k)")[:, 0:REL]
        vf = [relv[:, i * 4 * H:(i + 1) * 4 * H, :] for i in range(2)] \
            + [x0[:, 0:TC // 2].rearrange("p t b x -> p (t b x)").rearrange("p (h d) -> p h d", d=DH)]

        ps = [ctx.enter_context(nc.psum_tensor(f"bank{i}", [P, BANK], F32)) for i in range(8)]

        s_scan_in = sem("scan_inputs_loaded")
        s_rel_in = sem("relative_tables_loaded")
        s_rel = sem("relative_table_chain")
        s_rkp = sem("relative_key_parts_ready")
        s_rkw = sem("relative_key_parts_written")
        s_rks = sem("relative_key_stack_loaded")
        s_att_in = sem("attention_weights_loaded")
        s_leak = sem("leak_ready")
        s_gpre = sem("gate_sums_ready")
        s_gate = sem("gate_ready")
        s_hs = sem("states_kept")
        s_leaked = sem("leaked_state_ready")
        s_x0 = sem("paired_inputs_ready")
        s_pre = sem("tanh_input_ready")
        s_h = sem("state_ready")
        s_qps = sem("query_sums_ready")
        s_kps = sem("key_sums_ready")
        s_qf = sem("queries_copied")
        s_kf = sem("keys_copied")
        s_pc = sem("parts_chain")
        s_qp = sem("query_parts_ready")
        s_kp = sem("key_parts_ready")
        s_qw = [sem(f"query_parts_written{i}") for i in range(2)]
        s_qs = [sem(f"query_stack_loaded{i}") for i in range(2)]
        s_s2 = sem("relative_scores_ready")
        s_s2c = sem("relative_scores_copied")
        s_s2w = [sem(f"relative_scores_written{i}") for i in range(SETS)]
        s_full = sem("full_parts_written")
        s_vps = sem("value_sums_ready")
        s_vf = sem("values_copied")
        s_v0 = sem("value_first_parts_ready")
        s_vrest = sem("value_first_parts_subtracted")
        s_v1p = sem("value_second_parts_ready")
        s_pass = sem("gpsimd_wait_passed")
        s_spass = sem("sync_wait_passed")
        s_vp = sem("value_parts_ready")

        s2_out = s2_dram.rearrange("(g n) q k -> n g q k", g=NHG)
        PLINKS = 7
        QLINKS = 4

        def start1(r, j):
            return h1[r][:, j - 1, :] if j else h1[1 - r][:, TC - 1, :]

        def write_full(eng, dram, full):
            eng.dma_start(dram.rearrange("n p x -> p n x"), full[:].rearrange("p n b t -> p n (b t)"))\
               .then_inc(s_full, 16)

        VG = B // 4
        REL_LINKS = 9

        def v_part(g, n):
            return V27[:, 4 * g:4 * g + 4].rearrange("p b h n d -> p (b h) n d")[:, :, n, 0:DH]

        def macros(eng, step):
            step(0, 0, True, False, False)
            step(0, 1, True, True, False)
            with eng.Fori(1, NCH // 2) as i:
                for r in range(2):
                    step(i, r, True, True, True)
            step(NCH // 2, 0, False, True, True)
            step(NCH // 2, 1, False, False, True)

        with nc.Block() as block:
            @block.sync
            def _(sp):
                for r in range(2):
                    sp.sem_inc(s_qw[r], 16)
                for s in range(SETS):
                    sp.sem_inc(s_s2w[s], 16)
                for dst, src in ((wz[:], a["wz"]), (wh[:], a["wh"]), (h1[1][:, TC - 1, :], a["condT"]),
                                 (cols[:], a["cols"]), (xT[:], a["xT"])):
                    sp.dma_start(dst, src).then_inc(s_scan_in, 16)
                sp.dma_start(rk, a["relk"]).then_inc(s_rel_in, 16)
                win = bass.AP(a["relv"].tensor, 0, [[DH, P], [1, T * DH]])
                sp.dma_start(relv[:].rearrange("p q d -> p (q d)"), win).then_inc(s_rel_in, 16)
                for dst, src in ((wq[:], a["wq"]), (wk[:], a["wk"]), (wv[:], a["wv"]), (wo[:], a["wo"]),
                                 (wx2[:], a["wx2"]), (wh2[:], a["wh2"]),
                                 (ident[:], a["ident"]), (bv_bc[:], a["bv"].partition_broadcast(P))):
                    sp.dma_start(dst, src).then_inc(s_att_in, 16)
                sp.wait_ge(s_rkp, 1)
                for n in range(NP):
                    sp.dma_start(rk_dram[:, n].rearrange("j d x -> d j x"), rkp[:]).then_inc(s_rkw, 16)
                sp.wait_ge(s_rkw, 16 * NP)
                sp.dma_start(relkS[:], rk_dram.rearrange("j i d x -> (j i d) x")).then_inc(s_rks, 16)

                def write_scores(m, s):
                    c = m - 2
                    sp.wait_ge(s_s2c, c * TC + 4 * s + 4 + 4)
                    sp.sem_inc(s_spass, 1)
                    sp.dma_start(s2_out[:, :, bass.ds(c * TC + 4 * s, 4), :], stage[s][:]).then_inc(s_s2w[s], 16)

                def step(i, r, scan_on, proj_on, rel_on):
                    m = i * 2 + r
                    before = SETS // 2 if scan_on else 0
                    if rel_on:
                        for s in range(before):
                            write_scores(m, s)
                    if proj_on:
                        o = 1 - r
                        fill = i if r else i - 1
                        sp.wait_ge(s_qp, m + 1)
                        sp.sem_inc(s_spass, 1)
                        sp.dma_start(qtb_dram[bass.ds(m - 1, 1)].rearrange("c i p x -> (c p) i x"), qp[o][:])\
                          .then_inc(s_qw[o], 16)
                        sp.wait_ge(s_qw[o], fill * 16 + 32)
                        sp.sem_inc(s_spass, 1)
                        if rel_on:
                            sp.wait_ge(s_s2, (m - 2) * TC + 1)
                        sp.sem_inc(s_spass, 1)
                        for n in range(NP):
                            sp.dma_start(QS2[o][n * NP * DH:(n + 1) * NP * DH], qtb_dram[bass.ds(m - 1, 1)].rearrange(
                                "c i (d h) x -> (c i d) h x", h=H)).then_inc(s_qs[o], 16)
                    if proj_on and not scan_on:
                        sp.wait_ge(s_pc, PLINKS * (NCH - 1) + QLINKS)
                        write_full(sp, qbt_dram, qfull)
                    if rel_on:
                        for s in range(before, SETS):
                            write_scores(m, s)

                macros(sp, step)
                for s in range(SETS):
                    sp.wait_ge(s_s2w[s], 16 * NCH + 16)

            @block.tensor
            def _(pe):
                pe.sem_inc(s_s2, 1)
                pe.wait_ge(s_scan_in, 16 * 5)

                def project(w, bank, r, lo, n):
                    return pe.matmul(ps[bank][:, lo * B:(lo + n) * B], w[:], h1[1 - r][:, lo:lo + n, :],
                                     start=True, stop=True)

                def step(i, r, scan_on, proj_on, rel_on):
                    m = i * 2 + r
                    if proj_on and not rel_on:
                        pe.wait_ge(s_att_in, 16 * 8)
                        pe.wait_ge(s_rks, 16)
                    if proj_on and not scan_on:
                        pe.wait_ge(s_h, T + 1)
                        pe.wait_ge(s_qf, m)
                        project(wq, 2, r, 0, TC).then_inc(s_qps, 1)
                        pe.wait_ge(s_kf, m)
                        project(wk, 3, r, 0, TC).then_inc(s_kps, 1)
                        pe.wait_ge(s_hs, NCH)
                        for g in range(VG):
                            if g >= 2:
                                pe.wait_ge(s_vf, g - 1)
                            for j in range(4):
                                mm = pe.matmul(ps[g % 2][:, j * D:(j + 1) * D], hs[:, :, 4 * g + j], wv[:],
                                               start=True, stop=True)
                            mm.then_inc(s_vps, 1)
                    for j in range(TC):
                        if scan_on:
                            t = m * TC + j
                            pe.matmul(ps[j % 2][:, 0:B], wz[:], xT[:, bass.ds(t, 1), :], start=True, stop=False)
                            pe.wait_ge(s_h, t + 1)
                            pe.matmul(ps[j % 2][:, 0:B], wh[:], start1(r, j), start=False, stop=True)\
                              .then_inc(s_gpre, 1)
                            if proj_on and j < 8:
                                if j == 0:
                                    pe.wait_ge(s_qf, m)
                                if j == 4:
                                    pe.wait_ge(s_kf, m)
                                mm = project(wk if j >= 4 else wq, 2 + j // 4, r, 4 * (j % 4), 4)
                                if j % 4 == 3:
                                    mm.then_inc(s_kps if j >= 4 else s_qps, 1)
                        if rel_on:
                            c = m - 2
                            if j == 0:
                                pe.wait_ge(s_qs[r], i * (16 * NP))
                            pe.wait_ge(s_s2c, c * TC + j + 1)
                            for g in range(NHG):
                                mm = pe.matmul(ps[4 + j % 4][:, g * T:(g + 1) * T],
                                               QS2[r][:, 4 * g:4 * g + 4, j::TC],
                                               relk_window(c, j), start=True, stop=True)
                            mm.then_inc(s_s2, 1)

                def relk_window(c, j):
                    return relkS[:, bass.ds(c * (-TC) + (T - 1 - j), T)]

                macros(pe, step)

            @block.scalar
            def _(act):
                act.sem_inc(s_h, 1)
                act.sem_inc(s_qf, 1)
                act.sem_inc(s_kf, 1)
                act.preload_act_table_set("sigmoid_and_others")
                act.wait_ge(s_scan_in, 16 * 5)

                def step(i, r, scan_on, proj_on, rel_on):
                    m = i * 2 + r
                    for j in range(TC):
                        if scan_on:
                            t = m * TC + j
                            act.wait_ge(s_gpre, t + 1)
                            act.activation(gl[:, :, 0], ps[j % 2][:, 0:B], ACT.Sigmoid, bias=cols[:, 0:1])\
                               .then_inc(s_gate, 1)
                            act.wait_ge(s_pre, t + 1)
                            act.activation(h1[r][:, j, :], pre[:, :, 1], ACT.Tanh)\
                               .then_inc(s_h, 1)
                        if proj_on and j == 4:
                            act.wait_ge(s_qps, m)
                            act.wait_ge(s_qp, m)
                            act.activation(qf[:].rearrange("p b t -> p t b"),
                                           ps[2][:].rearrange("p (t b) -> p t b", b=B), ACT.Identity,
                                           bias=cols[:, 2:3]).then_inc(s_qf, 1)
                        if proj_on and j == 8:
                            act.wait_ge(s_kps, m)
                            act.wait_ge(s_kp, m)
                            act.activation(kf[:].rearrange("p b t -> p t b"),
                                           ps[3][:].rearrange("p (t b) -> p t b", b=B), ACT.Identity,
                                           bias=cols[:, 3:4]).then_inc(s_kf, 1)
                    if proj_on and not scan_on:
                        act.wait_ge(s_rel, REL_LINKS)
                        for s in range(VG + 1):
                            if s < VG:
                                act.wait_ge(s_vf, s + 1)
                                act.activation(v_part(s, 0), vf[s % 3], ACT.Copy).then_inc(s_v0, 1)
                            if s >= 1:
                                act.wait_ge(s_vrest, s)
                                act.activation(v_part(s - 1, 1), vf[(s - 1) % 3], ACT.Copy).then_inc(s_v1p, 1)

                macros(act, step)
                act.wait_ge(s_kp, NCH + 1)
                act.wait_ge(s_pc, PLINKS * NCH)
                write_full(act, kbt_dram, kfull)
                act.wait_ge(s_full, 32)

            @block.vector
            def _(dve):
                dve.sem_inc(s_s2c, 4)
                dve.wait_ge(s_scan_in, 16 * 5)
                dve.tensor_scalar(leak[:], cols[:, 1:2], -1.0, 1.0, ALU.mult, ALU.add).then_inc(s_leak, 1)
                dve.wait_ge(s_leak, 1)
                dve.memset(x0[:, :, :, 0], 0.0)

                def keep(m, r):
                    dve.tensor_scalar(hs[:, bass.ds((m - 1) * TC, TC), :], h1[1 - r][:], 1.0, None, ALU.mult)\
                        .then_inc(s_hs, 1)

                def step(i, r, scan_on, proj_on, rel_on):
                    m = i * 2 + r
                    if proj_on and not rel_on:
                        dve.wait_ge(s_rkp, 1)
                    if proj_on and not scan_on:
                        dve.wait_ge(s_h, T + 1)
                        keep(m, r)
                        dve.wait_ge(s_rel, REL_LINKS)
                        for s in range(VG + 2):
                            if s < VG:
                                dve.wait_ge(s_vps, s + 1)
                                dve.tensor_tensor(vf[s % 3].rearrange("p (b h) d -> p b (h d)", b=4),
                                                  ps[s % 2][:].rearrange("p (b e) -> p b e", b=4),
                                                  bv_bc[:].unsqueeze(1).broadcast_to([P, 4, D]), ALU.add)\
                                    .then_inc(s_vf, 1)
                            if 1 <= s <= VG:
                                g = s - 1
                                dve.wait_ge(s_v0, g + 1)
                                dve.tensor_tensor(vf[g % 3], vf[g % 3], v_part(g, 0), ALU.subtract)\
                                    .then_inc(s_vrest, 1)
                            if s >= 2:
                                g = s - 2
                                dve.wait_ge(s_v1p, g + 1)
                                dve.tensor_tensor(v_part(g, 2), vf[g % 3], v_part(g, 1), ALU.subtract)\
                                    .then_inc(s_vp, 1)
                                dve.wait_ge(s_vp, g + 1)
                    for j in range(TC):
                        if scan_on:
                            t = m * TC + j
                            dve.wait_ge(s_h, t + 1)
                            if j == 0:
                                dve.tensor_scalar(x0[:, :, :, 1], xT[:, bass.ds(t, TC), :], 1.0, None, ALU.mult)\
                                    .then_inc(s_x0, 1)
                                dve.wait_ge(s_x0, m + 1)
                            dve.tensor_scalar(gl[:, :, 1], start1(r, j), leak[:, 0:1], None,
                                              ALU.mult).then_inc(s_leaked, 1)
                            dve.wait_ge(s_leaked, t + 1)
                            dve.wait_ge(s_gate, t + 1)
                            dve.tensor_tensor_scan(pre[:].rearrange("p b x -> p (b x)"),
                                                   x0[:, j].rearrange("p b x -> p (b x)"),
                                                   gl[:].rearrange("p b x -> p (b x)"), 0.0, ALU.mult, ALU.add)\
                                .then_inc(s_pre, 1)
                        if proj_on and scan_on and j == 0:
                            keep(m, r)
                        if rel_on:
                            c = m - 2
                            dve.wait_ge(s_s2, c * TC + j + 2)
                            if j % 4 == 0:
                                dve.wait_ge(s_s2w[j // 4], c * 16 + 16)
                            dve.tensor_copy(stage[j // 4][:, :, j % 4, :],
                                            ps[4 + j % 4][:].rearrange("p (g k) -> p g k", k=T)).then_inc(s_s2c, 1)

                macros(dve, step)

            @block.gpsimd
            def _(pool):
                pool.sem_inc(s_qp, 1)
                pool.sem_inc(s_kp, 1)

                def split(parts, rest, link, last):
                    link(pool.tensor_copy(parts[0], rest))
                    link(pool.tensor_tensor(rest, rest, parts[0], ALU.subtract))
                    link(pool.tensor_copy(parts[1], rest))
                    last(pool.tensor_tensor(parts[2], rest, parts[1], ALU.subtract))

                n_rel = [0]

                def rel_link(op):
                    n_rel[0] += 1
                    op.then_inc(s_rel, 1)
                    pool.wait_ge(s_rel, n_rel[0])

                pool.wait_ge(s_rel_in, 32)
                split([rkp[:, n, :] for n in range(NP)], rk, rel_link, lambda op: op.then_inc(s_rkp, 1))
                for t9 in (V27[:].rearrange("p b h n d -> p (b h) n d"), relv27[:]):
                    pool.memset(t9[:, :, 0, DH:], 1.0)
                    rel_link(pool.memset(t9[:, :, 1:, DH:], 0.0))
                split([relv27[:, :, n, 0:DH] for n in range(NP)], relv[:], rel_link, rel_link)
                assert n_rel[0] == REL_LINKS

                def step(i, r, scan_on, proj_on, rel_on):
                    if not proj_on:
                        return
                    m = i * 2 + r
                    o = 1 - r
                    fill = i if r else i - 1
                    ts = bass.ds((m - 1) * TC, TC)
                    n = [0]

                    def link(op):
                        n[0] += 1
                        op.then_inc(s_pc, 1)
                        pool.wait_ge(s_pc, (m - 1) * PLINKS + n[0])
                        pool.sem_inc(s_pass, 1)

                    pool.wait_ge(s_qf, m + 1)
                    pool.wait_ge(s_qw[o], fill * 16 + 16)
                    pool.sem_inc(s_pass, 1)
                    split([qp[o][:, x, :] for x in range(NP)], qf[:].rearrange("p b t -> p (b t)"), link,
                          lambda op: op.then_inc(s_qp, 1))
                    pool.wait_ge(s_qp, m + 1)
                    pool.sem_inc(s_pass, 1)
                    link(pool.tensor_copy(qfull[:, :, :, ts], qp[o][:].rearrange("p i (b t) -> p i b t", t=TC)))
                    pool.wait_ge(s_kf, m + 1)
                    pool.sem_inc(s_pass, 1)
                    split([kfull[:, x, :, ts] for x in range(NP)], kf[:], link, lambda op: op.then_inc(s_kp, 1))
                    assert n[0] == PLINKS

                macros(pool, step)
        scan.close()

        with ExitStack() as st4:
            def sb4(name, shape, dt=F32):
                return st4.enter_context(nc.sbuf_tensor(name, shape, dt))

            HH = H // 2
            NU = 2 * GB
            RING = 4
            LEAD = 3
            PAIRS = GB // 2
            PSCALE = 1024.0
            PTh = sb4("PTh", [P, P, T], F16)
            PTl = sb4("PTl", [P, P, T], F16)
            pf = [sb4(f"pf{i}", [P, BANK]) for i in range(2)]
            QS = [sb4(f"QS{i}", [KS, H, 2 * T], BF16) for i in range(2)]
            KSt = [sb4(f"KS{i}", [KS, H, 2 * T], BF16) for i in range(2)]
            s2t = [sb4(f"s2t{i}", [P, HH, T]) for i in range(RING)]
            sc = [sb4(f"sc{i}", [P, HH, T]) for i in range(RING)]
            mx = [sb4(f"mx{i}", [P, HH]) for i in range(RING)]
            wsum = [sb4(f"wsum{i}", [P, H, DH + 1]) for i in range(2)]
            wnorm = [sb4(f"wnorm{i}", [P, H, DH]) for i in range(2)]
            wrec = [sb4(f"wrec{i}", [P, H]) for i in range(2)]
            QC = H
            NQC = T // QC
            w2s = [sb4(f"w2s{i}", [P, P]) for i in range(2)]

            s_qks = [sem(f"operand_stacks_loaded{i}") for i in range(2)]
            s_s1 = sem("content_scores_ready")
            s_s2l = [sem(f"relative_scores_loaded{i}") for i in range(RING)]
            s_add = sem("scores_summed")
            s_max = sem("row_maxima_ready")
            s_sub = sem("maxima_subtracted")
            s_exp = sem("exp_ready")
            s_tr = sem("exp_transposed")
            s_pth = sem("first_parts_ready")
            s_ptl = sem("second_parts_ready_vector")
            s_pf = sem("transposed_numerators_copied")
            s_ptp = sem("second_parts_ready_gpsimd")
            s_w1 = sem("value_product_ready")
            s_v1 = sem("value_product_chain")
            s_w1n = sem("value_product_normalised")
            s_w1t = sem("value_product_transposed")
            s_w1c = sem("value_product_stored")
            s_w2 = sem("relative_value_product_ready")
            s_v2 = sem("relative_value_product_chain")
            s_w2n = sem("relative_value_product_normalised")
            s_w2t = sem("relative_value_product_transposed")
            s_w2c = sem("relative_value_product_copied")
            s_w2d = [sem(f"relative_value_product_written{i}") for i in range(2)]
            s2_in = s2_dram.rearrange("(h p r) q k -> q h p r k", h=H, r=2)
            PRIME = 2 * 4

            with nc.Block() as block:
                @block.sync
                def _(sp):
                    def load_stacks(g, p):
                        at = bass.ds((g * PAIRS + p) * (2 * T), 2 * T)
                        for j in range(NP):
                            rows = slice(j * NP * DH, (j + 1) * NP * DH)
                            sp.dma_start(QS[p % 2][rows], qbt_dram[:, :, at].rearrange("i (d h) x -> (i d) h x", h=H))\
                              .then_inc(s_qks[p % 2], 16)
                            key = kbt_dram[j:j + 1, :, at].rearrange("j (d h) x -> j d h x", h=H)
                            sp.dma_start(KSt[p % 2][rows], key.broadcast_to([NP, DH, H, 2 * T]))\
                              .then_inc(s_qks[p % 2], 16)

                    with sp.Fori(0, 2) as gp:
                        with sp.Fori(0, 2) as gm:
                            g = gp * 2 + gm
                            for u in range(NU):
                                if u % 4 == 0:
                                    sp.wait_ge(s_s1, g * NU + (u - 4 + PRIME))
                                    sp.sem_inc(s_spass, 1)
                                    load_stacks(g, u // 4)
                                sp.wait_ge(s_add, g * NU + u + 1)
                                sp.sem_inc(s_spass, 1)
                                half = u % 2
                                src = s2_in[:, bass.ds(gm * GB + u // 2, 1), half * HH:(half + 1) * HH,
                                            bass.ds(gp, 1), :]
                                sp.dma_start(s2t[u % RING][:], src.rearrange("q a p r k -> q (a p r) k"))\
                                  .then_inc(s_s2l[u % RING], 16)

                @block.gpsimd
                def _(pool):
                    pool.sem_inc(s_ptp, 2)

                    def shift(g, u):
                        pool.wait_ge(s_max, g * NU + u + 1)
                        pool.tensor_tensor(sc[u % RING][:], sc[u % RING][:],
                                           mx[u % RING][:].unsqueeze(2).broadcast_to([P, HH, T]), ALU.subtract)\
                            .then_inc(s_sub, 1)

                    def group(g, last):
                        for s in range(NU):
                            rows = slice(s * HH + 4, s * HH + 8)
                            pool.wait_ge(s_pf, g * NU + s + 1)
                            pool.tensor_tensor(PTl[:, rows, :].rearrange("p h q -> p (h q)"), pf[s % 2][:],
                                               PTh[:, rows, :].rearrange("p h q -> p (h q)"), ALU.subtract)\
                                .then_inc(s_ptp, 1)
                            if s < NU - LEAD:
                                shift(g, s + LEAD)
                            elif not last:
                                shift(g + 1, s + LEAD - NU)

                    for u in range(LEAD):
                        shift(0, u)
                    with pool.Fori(0, NG - 1) as g:
                        group(g, last=False)
                    group(NG - 1, last=True)

                @block.tensor
                def _(pe):
                    pe.sem_inc(s_s1, PRIME)
                    pe.sem_inc(s_tr, 2 * RING)
                    pe.sem_inc(s_w2, 1)

                    def content_scores(g, u):
                        bl, half = u // 2, u % 2
                        if u % 4 == 0:
                            p = bl // 2
                            pe.wait_ge(s_qks[p % 2], (g * (PAIRS // 2) + p // 2 + 1) * (32 * NP))
                        pe.wait_ge(s_add, g * NU + u - 1 + RING)
                        x = slice(bl % 2 * T, (bl % 2 + 1) * T)
                        for h in range(HH):
                            mm = pe.matmul(ps[2 * (u % 2) + h // 4][:, h % 4 * T:(h % 4 + 1) * T],
                                           QS[bl // 2 % 2][:, half * HH + h, x],
                                           KSt[bl // 2 % 2][:, half * HH + h, x], start=True, stop=True)
                        mm.then_inc(s_s1, 1)

                    def group(g, last):
                        pe.wait_ge(s_w2n, g * NQC + 1)
                        for s in range(NU + 4):
                            if s < NU - LEAD:
                                content_scores(g, s + LEAD)
                            elif s < NU and not last:
                                content_scores(g + 1, s + LEAD - NU)
                            if s < NU:
                                pe.wait_ge(s_exp, g * NU + s + 1)
                                for x in range(2):
                                    if s and not x:
                                        pe.wait_ge(s_ptl, g * NU + s + 1)
                                    if s and x:
                                        pe.wait_ge(s_pf, g * NU + s)
                                    for j in range(4):
                                        mm = pe.transpose(ps[4 + x][:, j * T:(j + 1) * T],
                                                          sc[s % RING][:, 4 * x + j, :], ident[:])
                                    mm.then_inc(s_tr, 1)
                            if 3 <= s < NU + 2 and s % 2:
                                bl = (s - 3) // 2
                                if bl == 0:
                                    pe.wait_ge(s_w2c, g * NQC + 1)
                                pe.wait_ge(s_ptl, g * NU + s)
                                pe.wait_ge(s_ptp, g * NU + s + 1)
                                pe.wait_ge(s_w1n, g * GB + bl + 1)
                                for h in range(H):
                                    for part in (PTh, PTl):
                                        mm = pe.matmul(ps[6][:, h * VW:(h + 1) * VW], part[:, bl * H + h, :],
                                                       V27[:, bass.ds(g * GB + bl, 1), h].rearrange(
                                                           "p b n d -> p (b n d)"),
                                                       start=(part is PTh), stop=(part is PTl))
                                mm.then_inc(s_w1, 1)
                            if s >= 5 and s % 2:
                                bl = (s - 5) // 2
                                pe.wait_ge(s_w1n, g * GB + bl + 2)
                                pe.wait_ge(s_w1c, g * GB + bl + 1)
                                pe.transpose(ps[7][:, 0:T], wnorm[bl % 2][:].rearrange("p h d -> p (h d)"), ident[:])\
                                  .then_inc(s_w1t, 1)
                        for c in range(NQC + 2):
                            if c < NQC:
                                if c == 0:
                                    pe.wait_ge(s_add, (g + 1) * NU + (0 if last else LEAD) + RING)
                                elif c >= 4:
                                    pe.wait_ge(s_w2n, g * NQC + c - 2)
                                for j in range(QC):
                                    q = QC * c + j
                                    for part in (PTh, PTl):
                                        mm = pe.matmul(ps[c % 4][:, j * VW:(j + 1) * VW], part[:, :, q],
                                                       relv27[:, T - 1 - q].rearrange("p n d -> p (n d)"),
                                                       start=(part is PTh), stop=(part is PTl))
                                mm.then_inc(s_w2, 1)
                            if c >= 2:
                                n = c - 2
                                pe.wait_ge(s_w2n, g * NQC + c)
                                if n >= 2:
                                    pe.wait_ge(s_w2c, g * NQC + n)
                                else:
                                    pe.wait_ge(s_w1c, g * GB + GB + 1)
                                pe.transpose(ps[6 + n % 2][:, 0:P], wnorm[n % 2][:].rearrange("p q d -> p (q d)"),
                                             ident[:]).then_inc(s_w2t, 1)

                    for u in range(LEAD):
                        content_scores(0, u)
                    with pe.Fori(0, NG - 1) as g:
                        group(g, last=False)
                    group(NG - 1, last=True)

                @block.vector
                def _(dve):
                    dve.sem_inc(s_add, RING)
                    dve.sem_inc(s_w1n, 1)
                    dve.sem_inc(s_ptl, 1)
                    dve.sem_inc(s_w2n, 1)

                    def normalise(s_chain, links, bank, n, summed, rec, out, ready):
                        parts = ps[bank][:, 0:n * VW].rearrange("p (n x d) -> p n d x", x=NP, d=DH + 1)
                        dve.tensor_reduce(summed[:], parts, AX.X, ALU.add).then_inc(s_chain, 1)
                        dve.wait_ge(s_chain, links + 1)
                        dve.reciprocal(rec[:].unsqueeze(2), summed[:, :, DH:]).then_inc(s_chain, 1)
                        dve.wait_ge(s_chain, links + 2)
                        dve.tensor_tensor(out[:], summed[:, :, 0:DH], rec[:].unsqueeze(2).broadcast_to([P, n, DH]),
                                          ALU.mult).then_inc(ready, 1)

                    def scores(g, u):
                        r = u % RING
                        dve.wait_ge(s_s1, g * NU + u + 1 + PRIME)
                        dve.wait_ge(s_s2l[r], (g * (NU // RING) + u // RING + 1) * 16)
                        dve.wait_ge(s_tr, (g * NU + u + 1) * 2)
                        for x in range(2):
                            op = dve.tensor_tensor(sc[r][:, 4 * x:4 * x + 4, :],
                                                   ps[2 * (u % 2) + x][:].rearrange("p (h k) -> p h k", k=T),
                                                   s2t[r][:, 4 * x:4 * x + 4, :], ALU.add)
                        op.then_inc(s_add, 1)
                        dve.wait_ge(s_add, g * NU + u + 1 + RING)
                        dve.tensor_reduce(mx[r][:], sc[r][:], AX.X, ALU.max).then_inc(s_max, 1)

                    def group(g, last):
                        for s in range(NU + 3):
                            if s >= 4 and s % 2 == 0:
                                bl = (s - 4) // 2
                                dve.wait_ge(s_w1, g * GB + bl + 1)
                                if bl >= 2:
                                    dve.wait_ge(s_w1t, g * GB + bl - 1)
                                normalise(s_v1, (g * GB + bl) * 2, 6, H, wsum[bl % 2], wrec[bl % 2], wnorm[bl % 2],
                                          s_w1n)
                            if s < NU - LEAD:
                                scores(g, s + LEAD)
                            elif s < NU and not last:
                                scores(g + 1, s + LEAD - NU)
                            if s < NU:
                                rows = slice(s * HH, s * HH + 4)
                                dve.wait_ge(s_pth, (g * NU + s) * 2 + 1)
                                dve.scalar_tensor_tensor(out=PTl[:, rows, :].rearrange("p h q -> p (h q)"),
                                                         in0=ps[4][:], scalar=PSCALE,
                                                         in1=PTh[:, rows, :].rearrange("p h q -> p (h q)"),
                                                         op0=ALU.mult, op1=ALU.subtract).then_inc(s_ptl, 1)
                        for c in range(NQC):
                            dve.wait_ge(s_w2, g * NQC + c + 2)
                            if c < 2:
                                dve.wait_ge(s_w1t, g * GB + GB - 1 + c)
                            if c >= 2:
                                dve.wait_ge(s_w2t, g * NQC + c - 1)
                            normalise(s_v2, (g * NQC + c) * 2, c % 4, QC, wsum[c % 2], wrec[c % 2], wnorm[c % 2], s_w2n)

                    for u in range(LEAD):
                        scores(0, u)
                    with dve.Fori(0, NG - 1) as g:
                        group(g, last=False)
                    group(NG - 1, last=True)

                @block.scalar
                def _(act):
                    act.sem_inc(s_w2c, 1)
                    act.sem_inc(s_w1c, 1)
                    for r in range(2):
                        act.sem_inc(s_w2d[r], 16)
                    act.preload_act_table_set("exp_and_others")

                    def numerators(g, u):
                        act.wait_ge(s_sub, g * NU + u + 1)
                        act.activation(sc[u % RING][:], sc[u % RING][:], ACT.Exp, scale=DH ** -0.5).then_inc(s_exp, 1)

                    def group(g, last):
                        for s in range(NU + 4):
                            for x in range(2):
                                if s >= NU:
                                    break
                                act.wait_ge(s_tr, (g * NU + s + RING) * 2 + x + 1)
                                if s == 0 and x == 0:
                                    act.wait_ge(s_w2, g * NQC + 1)
                                act.activation(PTh[:, s * HH + 4 * x:s * HH + 4 * x + 4, :],
                                               ps[4 + x][:].rearrange("p (h q) -> p h q", q=T), ACT.Copy,
                                               scale=PSCALE).then_inc(s_pth, 1)
                            if s < NU:
                                act.wait_ge(s_ptp, g * NU + s + 1)
                                act.activation(pf[s % 2][:], ps[5][:], ACT.Copy, scale=PSCALE).then_inc(s_pf, 1)
                            if s < NU - LEAD + 1:
                                numerators(g, s + LEAD - 1)
                            elif s < NU and not last:
                                numerators(g + 1, s + LEAD - 1 - NU)
                            if s >= 5 and s % 2:
                                bl = (s - 5) // 2
                                act.wait_ge(s_w1t, g * GB + bl + 1)
                                act.activation(OT1[:, bass.ds(g * GB + bl, 1), :], ps[7][:, 0:T].unsqueeze(1),
                                               ACT.Copy).then_inc(s_w1c, 1)
                        for n in range(NQC):
                            act.wait_ge(s_w2t, g * NQC + n + 1)
                            act.wait_ge(s_w2d[n % 2], (g * (NQC // 2) + n // 2) * 16 + 16)
                            act.activation(w2s[n % 2][:], ps[6 + n % 2][:, 0:P], ACT.Copy).then_inc(s_w2c, 1)
                            act.wait_ge(s_w2c, g * NQC + n + 2)
                            act.dma_start(w2_dram[n * P:(n + 1) * P, bass.ds(g * P, P)], w2s[n % 2][:])\
                               .then_inc(s_w2d[n % 2], 16)

                    for u in range(LEAD - 1):
                        numerators(0, u)
                    with act.Fori(0, NG - 1) as g:
                        group(g, last=False)
                    group(NG - 1, last=True)
                    for r in range(2):
                        act.wait_ge(s_w2d[r], 16 * NG * (NQC // 2) + 16)
        att.close()

        x1r = sb("x1r", [P, NT, D])
        with ExitStack() as st5:
            OT2 = st5.enter_context(nc.sbuf_tensor("OT2", [P, T, B], F32))
            s_ot2 = sem("relative_value_outputs_loaded")
            s_y = sem("output_projection_ready")
            s_x1 = sem("residual_ready")
            s_x1t = sem("residual_transposed")
            s_x1r = sem("residual_rows_ready")
            w2_in = w2_dram.rearrange("(q d) (h b) -> h d q b", d=DH, b=B)
            with nc.Block() as block:
                @block.sync
                def _(sp):
                    for h in range(0, H, 2):
                        sp.dma_start(OT2[h * DH:(h + 1) * DH, :, :], w2_in[h]).then_inc(s_ot2, 16)

                @block.scalar
                def _(act):
                    for h in range(1, H, 2):
                        act.dma_start(OT2[h * DH:(h + 1) * DH, :, :], w2_in[h]).then_inc(s_ot2, 16)
                    for c in range(NCH):
                        act.wait_ge(s_x1t, c + 1)
                        act.activation(x1r[:, c * JT:(c + 1) * JT, :], ps[c][:].rearrange("p (j d) -> p j d", d=D),
                                       ACT.Copy).then_inc(s_x1r, 1)

                @block.tensor
                def _(pe):
                    for c in range(NCH):
                        pe.matmul(ps[c][:], wo[:], OT1[:, :, c * TC:(c + 1) * TC].rearrange("p b t -> p t b"),
                                  start=True, stop=False)
                    pe.wait_ge(s_ot2, 16 * H)
                    for c in range(NCH + 1):
                        if c < NCH:
                            pe.matmul(ps[c][:], wo[:], OT2[:, c * TC:(c + 1) * TC, :], start=False, stop=True)\
                              .then_inc(s_y, 1)
                        if c >= 1:
                            n = c - 1
                            pe.wait_ge(s_x1, n + 1)
                            x1 = xT[:, n * TC:(n + 1) * TC, :].rearrange("p t b -> p (t b)")
                            for j in range(JT):
                                mm = pe.transpose(ps[n][:, j * P:(j + 1) * P], x1[:, j * P:(j + 1) * P], ident[:])
                            mm.then_inc(s_x1t, 1)

                @block.vector
                def _(dve):
                    for c in range(NCH):
                        ts = slice(c * TC, (c + 1) * TC)
                        dve.wait_ge(s_y, c + 1)
                        dve.scalar_tensor_tensor(out=xT[:, ts, :].rearrange("p t b -> p (t b)"), in0=ps[c][:],
                                                 scalar=cols[:, 4:5], in1=xT[:, ts, :].rearrange("p t b -> p (t b)"),
                                                 op0=ALU.add, op1=ALU.add).then_inc(s_x1, 1)

        xg_dram = nc.dram_tensor("expert_inputs", (E * CAP + NULL * P, D + 1), F32).ap()
        yg_dram = nc.dram_tensor("expert_outputs", (2 * N + (E + NULL) * P, D), F32).ap()
        h2 = [sb(f"h2_{i}", [P, TC, B]) for i in range(2)]
        w1a = sb("w1a", [P, E, FF + FC])
        w2all = sb("w2all", [P, E, FC * D + D])
        rwT = sb("rwT", [P, E])
        upper = sb("upper", [P, P])
        ones = sb("ones", [P, P])
        iota = sb("iota", [P, E])
        ebase = sb("ebase", [P, E])
        mult = sb("mult", [P, MT])
        tri = sb("tri", [P, E, E])
        tiles = sb("tiles", [P, NS])
        padid = sb("padid", [P, E + NULL])
        destf = sb("destf", [P, 2 * JT])
        pad = sb("pad", [P, E + NULL, D + 1])
        wts = sb("wts", [P, 2, NT])
        tab = sb("tab", [P, 2, NS], I32)
        tabf = sb("tabf", [P, 2, NS])
        ends = sb("ends", [P, E], I32)
        cnt = sb("cnt", [P, E])
        ge = sb("ge", [P, NS, E])
        gm = sb("gm", [P, NS, E])
        gt = sb("gt", [P, E, MT])
        nt = sb("nt", [P, E])
        nte = sb("nte", [P, E, E])
        cum = sb("cum", [P, E])
        adj = sb("adj", [P, E])
        rows = [sb(f"rows{i}", [P, 2 * JT, D + 1]) for i in range(2)]
        slotu = [sb(f"slotu{i}", [P, 2 * JT], U32) for i in range(2)]
        top = sb("top", [P, JT, 8])
        topi = sb("topi", [P, JT, 8], U32)
        topf = sb("topf", [P, JT, 8])
        lg = sb("lg", [P, JT, E])
        lgc = sb("lgc", [P, JT, E])
        ex = sb("ex", [P, JT, E])
        small = sb("small", [P, 4, JT])
        sel = sb("sel", [P, 2, JT, E])
        both = sb("both", [P, JT, E])
        exs = sb("exs", [P, 2, JT, E])
        er = sb("er", [P, 2, JT])
        pos = sb("pos", [P, JT, E])
        offs = sb("offs", [P, JT + 1, E])
        slotf = sb("slotf", [P, 2, JT])
        s_c2 = sem("scan2_state_loaded")
        s_rin = sem("router_inputs_loaded")
        s_win = sem("expert_weights_loaded")
        s_r = sem("scan2_sums_ready")
        s_h2 = sem("scan2_state_ready")
        s_pad = sem("padding_rows_ready")
        s_null = sem("unused_tiles_written")
        s_lg = sem("logits_ready")
        s_rt = sem("state_rows_ready")
        s_v = sem("routing_chain")
        s_ea = sem("router_shift_ready")
        s_eb = sem("router_exp_ready")
        s_sel = sem("choices_ready")
        s_pos = sem("positions_ready")
        s_slot = sem("rows_and_slots_ready")
        s_sc = sem("rows_scattered")
        s_scd = sem("chunk_scattered")
        s_slotf = sem("slot_numbers_ready")
        s_init = sem("routing_start_values_set")
        s_tab = sem("tile_table_ready")
        s_end = sem("expert_ends_ready")
        s_spass2 = sem("sync_ends_wait_passed")
        s_fill = sem("padding_scattered")
        s_rpass = sem("gpsimd_routing_wait_passed")
        VLINKS = 18

        def before(r, j):
            return h2[r][:, j - 1, :] if j else h2[1 - r][:, TC - 1, :]

        def steps2(eng, step):
            step(0, 0, True, False)
            step(0, 1, True, True)
            with eng.Fori(1, NCH // 2) as i:
                for r in range(2):
                    step(i, r, True, True)
            step(NCH // 2, 0, False, True)

        with nc.Block() as block:
            @block.sync
            def _(sp):
                sp.dma_start(h2[1][:, TC - 1, :], a["condT"]).then_inc(s_c2, 16)
                for dst, src in ((rwT[:], a["rwT"]), (upper[:], a["upper"]), 
                                 (iota[:], a["iota"].partition_broadcast(P)),
                                 (ebase[:], a["ebase"].partition_broadcast(P)),
                                 (mult[:], a["mult"].partition_broadcast(P)),
                                 (tri[:].rearrange("p a b -> p (a b)"), a["tri"].partition_broadcast(P)),
                                 (tiles[:], a["tiles"].partition_broadcast(P)),
                                 (padid[:], a["padid"]), (destf[:], a["dest"])):
                    sp.dma_start(dst, src).then_inc(s_rin, 16)
                sp.dma_start(w1a[:, :, 0:FF], a["w1T"]).then_inc(s_win, 16)
                sp.dma_start(w1a[:, :, FF:], a["b1c"]).then_inc(s_win, 16)
                sp.dma_start(w2all[:, :, 0:FC * D], a["w2T"].rearrange("p e f d -> p e (f d)")).then_inc(s_win, 16)
                for e in range(E):
                    sp.dma_start(w2all[:, e, FC * D:], a["b2"][e].partition_broadcast(P)).then_inc(s_win, 16)
                sp.wait_ge(s_pad, 1)
                sp.dma_start(xg_dram[E * CAP:, :].rearrange("(n p) w -> p n w", p=P), pad[:, E:, :])\
                  .then_inc(s_null, 16)
                sp.wait_ge(s_null, 16)
                sp.wait_ge(s_win, 16 * (3 + E))
                sp.wait_ge(s_end, 1)
                sp.sem_inc(s_spass2, 1)
                for e in range(E):
                    end = sp.value_load(ends[0:1, e:e + 1], min_val=0, max_val=E * CAP - P)
                    sp.dma_start(xg_dram[bass.ds(end, P), :], pad[:, e, :]).then_inc(s_fill, 16)
                sp.wait_ge(s_fill, 16 * E)

            @block.tensor
            def _(pe):
                pe.wait_ge(s_c2, 16)

                def step(i, r, scan_on, route_on):
                    m = i * 2 + r
                    o = 1 - r
                    if not scan_on:
                        pe.wait_ge(s_h2, T + 1)
                    if isinstance(m, int) and m == 1:
                        pe.wait_ge(s_rin, 144)
                        pe.wait_ge(s_init, 1)
                    for j in range(TC):
                        if scan_on:
                            t = m * TC + j
                            pe.matmul(ps[j % 2][:, 0:B], wx2[:], xT[:, bass.ds(t, 1), :], start=True, stop=False)
                            pe.wait_ge(s_h2, t + 1)
                            pe.matmul(ps[j % 2][:, 0:B], wh2[:], before(r, j), start=False, stop=True)\
                              .then_inc(s_r, 1)
                        if not route_on:
                            continue
                        c = m - 1
                        if 2 <= j < 2 + JT:
                            k = j - 2
                            if k == 0:
                                pe.wait_ge(s_slot, c + 1)
                            tile = h2[o][:].rearrange("p t b -> p (t b)")[:, k * P:(k + 1) * P]
                            mm = pe.matmul(ps[2][:, k * E:(k + 1) * E], tile, rwT[:], start=True, stop=True)
                            if k == JT - 1:
                                mm.then_inc(s_lg, 1)
                            mm = pe.transpose(ps[3][:, k * P:(k + 1) * P], tile, ident[:])
                            if k == JT - 1:
                                mm.then_inc(s_rt, 1)
                        if j == 10:
                            pe.wait_ge(s_sel, c + 1)
                            chosen = both[:].rearrange("p j e -> p (j e)")
                            pe.matmul(ps[4][:, 0:JT * E], upper[:], chosen, start=True, stop=True)
                            pe.matmul(ps[4][:, JT * E:2 * JT * E], ones[:], chosen, start=True, stop=True)\
                              .then_inc(s_pos, 1)

                steps2(pe, step)

            @block.scalar
            def _(act):
                act.sem_inc(s_h2, 1)
                act.preload_act_table_set("exp_and_others")
                act.wait_ge(s_c2, 16)

                def step(i, r, scan_on, route_on):
                    m = i * 2 + r
                    for j in range(TC):
                        if scan_on:
                            t = m * TC + j
                            act.wait_ge(s_r, t + 1)
                            act.activation(h2[r][:, j, :], ps[j % 2][:, 0:B], ACT.Tanh,
                                           bias=cols[:, 5:6]).then_inc(s_h2, 1)
                        if route_on and j == 9:
                            act.wait_ge(s_ea, m)
                            act.activation(ex[:], lg[:], ACT.Exp).then_inc(s_eb, 1)

                steps2(act, step)

            @block.gpsimd
            def _(pool):
                pool.sem_inc(s_scd, 2)
                pool.wait_ge(s_rin, 144)
                pool.memset(ones[:], 1.0)
                pool.memset(pad[:, :, 0:D], 0.0)
                pool.tensor_copy(pad[:, :, D].bitcast(U32), padid[:]).then_inc(s_pad, 1)

                def step(i, r, scan_on, route_on):
                    if not route_on:
                        return
                    m = i * 2 + r
                    c = m - 1
                    o = 1 - r
                    pool.wait_ge(s_slot, c + 2)
                    pool.sem_inc(s_rpass, 1)
                    for k in range(2 * JT):
                        pool.indirect_dma_start(xg_dram, bass.IndirectOffsetOnAxis(slotu[o][:, k:k + 1], 0),
                                                rows[o][:, k, :], None).then_inc(s_sc, 16)
                    pool.wait_ge(s_sc, (c + 1) * (16 * 2 * JT))
                    pool.sem_inc(s_scd, 1)

                steps2(pool, step)

            @block.vector
            def _(dve):
                dve.sem_inc(s_slot, 1)
                dve.wait_ge(s_rin, 144)
                dve.wait_ge(s_pad, 1)
                dve.tensor_copy(offs[:, 0, :], ebase[:]).then_inc(s_init, 1)
                dve.wait_ge(s_init, 1)

                def step(i, r, scan_on, route_on):
                    if not route_on:
                        return
                    m = i * 2 + r
                    c = m - 1
                    o = 1 - r
                    k = [0]

                    def link(op):
                        k[0] += 1
                        op.then_inc(s_v, 1)
                        dve.wait_ge(s_v, c * VLINKS + k[0])

                    def over_e(v):
                        return v.unsqueeze(len(v.shape)).broadcast_to([*v.shape, E])

                    dve.wait_ge(s_lg, c + 1)
                    link(dve.tensor_copy(lgc[:], ps[2][:, 0:JT * E].rearrange("p (j e) -> p j e", e=E)))
                    dve.tensor_reduce(small[:, 0, :], lgc[:], AX.X, ALU.max)
                    for j in range(JT):
                        op = dve.max(top[:, j, :], lgc[:, j, :])
                    link(op)
                    dve.tensor_tensor(lg[:], lgc[:], over_e(small[:, 0, :]), ALU.subtract).then_inc(s_ea, 1)
                    for j in range(JT):
                        op = dve.max_index(topi[:, j, :], top[:, j, :], lgc[:, j, :])
                    link(op)
                    link(dve.tensor_copy(topf[:], topi[:]))
                    for x in range(2):
                        op = dve.tensor_tensor(sel[:, x], iota[:].unsqueeze(1).broadcast_to([P, JT, E]),
                                               topf[:, :, x:x + 1].broadcast_to([P, JT, E]), ALU.is_equal)
                    link(op)
                    dve.tensor_tensor(both[:], sel[:, 0], sel[:, 1], ALU.add).then_inc(s_sel, 1)
                    dve.wait_ge(s_rt, c + 1)
                    dve.wait_ge(s_scd, c + 1)
                    for x in range(2):
                        dve.tensor_copy(rows[o][:, x * JT:(x + 1) * JT, 0:D],
                                        ps[3][:].rearrange("p (j d) -> p j d", d=D))
                    link(dve.tensor_copy(rows[o][:, :, D].bitcast(U32), destf[:]))
                    link(dve.tensor_scalar(destf[:], destf[:], float(BANK), None, ALU.add))
                    dve.wait_ge(s_eb, c + 1)
                    dve.tensor_reduce(small[:, 0, :], ex[:], AX.X, ALU.add)
                    link(dve.tensor_tensor(exs[:], sel[:], ex[:].unsqueeze(1).broadcast_to([P, 2, JT, E]), ALU.mult))
                    link(dve.tensor_reduce(er[:], exs[:], AX.X, ALU.add))
                    link(dve.tensor_tensor(small[:, 1, :], er[:, 0], er[:, 1], ALU.add))
                    link(dve.scalar_tensor_tensor(out=small[:, 2, :], in0=small[:, 0, :], scalar=1e-9,
                                                  in1=small[:, 1, :], op0=ALU.mult, op1=ALU.add))
                    link(dve.reciprocal(small[:, 3, :], small[:, 2, :]))
                    dve.tensor_tensor(wts[:, :, bass.ds(c * JT, JT)], er[:],
                                      small[:, 3, :].unsqueeze(1).broadcast_to([P, 2, JT]), ALU.mult)
                    dve.wait_ge(s_pos, c + 1)
                    totals = ps[4][:, JT * E:2 * JT * E].rearrange("p (j e) -> p j e", e=E)
                    for j in range(JT):
                        link(dve.tensor_tensor(offs[:, j + 1, :], offs[:, j, :], totals[:, j, :], ALU.add))
                    link(dve.tensor_tensor(pos[:], ps[4][:, 0:JT * E].rearrange("p (j e) -> p j e", e=E),
                                           offs[:, 0:JT, :], ALU.add))
                    dve.tensor_copy(offs[:, 0, :], offs[:, JT, :])
                    link(dve.tensor_tensor(exs[:], sel[:], pos[:].unsqueeze(1).broadcast_to([P, 2, JT, E]), ALU.mult))
                    assert k[0] == VLINKS, k
                    dve.tensor_reduce(slotf[:], exs[:], AX.X, ALU.add).then_inc(s_slotf, 1)
                    dve.wait_ge(s_slotf, c + 1)
                    dve.tensor_copy(slotu[o][:], slotf[:].rearrange("p x j -> p (x j)")).then_inc(s_slot, 1)
                    dve.wait_ge(s_slot, c + 2)

                steps2(dve, step)

                n = [0]

                def tlink(op):
                    n[0] += 1
                    op.then_inc(s_tab, 1)
                    dve.wait_ge(s_tab, n[0])

                dve.tensor_copy(ends[:], offs[:, 0, :]).then_inc(s_end, 1)
                tlink(dve.tensor_tensor(cnt[:], offs[:, 0, :], ebase[:], ALU.subtract))
                tlink(dve.tensor_tensor(gt[:], cnt[:].unsqueeze(2).broadcast_to([P, E, MT]),
                                        mult[:].unsqueeze(1).broadcast_to([P, E, MT]), ALU.is_gt))
                tlink(dve.tensor_reduce(nt[:], gt[:], AX.X, ALU.add))
                dve.tensor_scalar(adj[:], nt[:], float(-P), float(CAP), ALU.mult, ALU.add)
                tlink(dve.tensor_tensor(nte[:], tri[:], nt[:].unsqueeze(1).broadcast_to([P, E, E]), ALU.mult))
                tlink(dve.tensor_reduce(cum[:], nte[:], AX.X, ALU.add))
                tlink(dve.tensor_tensor(ge[:], tiles[:].unsqueeze(2).broadcast_to([P, NS, E]),
                                        cum[:].unsqueeze(1).broadcast_to([P, NS, E]), ALU.is_ge))
                tlink(dve.tensor_tensor(gm[:], ge[:], adj[:].unsqueeze(1).broadcast_to([P, NS, E]), ALU.mult))
                dve.tensor_reduce(tabf[:, 0, :], ge[:], AX.X, ALU.add)
                tlink(dve.tensor_reduce(tabf[:, 1, :], gm[:], AX.X, ALU.add))
                dve.tensor_scalar(tabf[:, 0, :], tabf[:, 0, :], float(E - 1), None, ALU.min)
                tlink(dve.scalar_tensor_tensor(out=tabf[:, 1, :], in0=tiles[:], scalar=float(P), in1=tabf[:, 1, :],
                                               op0=ALU.mult, op1=ALU.add))
                tlink(dve.tensor_copy(tab[:], tabf[:]))

        RX = 8
        xr = [sb(f"xr{i}", [P, D + 1]) for i in range(RX)]
        yr = [sb(f"yr{i}", [P, D]) for i in range(RX)]
        xt = [sb(f"xt{i}", [P, P]) for i in range(2)]
        w1b = [sb(f"w1b{i}", [P, FF + FC]) for i in range(2)]
        w2b = [sb(f"w2b{i}", [P, FC * D + D]) for i in range(2)]
        hid = [sb(f"hid{i}", [P, FC, P]) for i in range(2)]
        s_xr = [sem(f"tile_rows_loaded{i}") for i in range(RX)]
        s_ys = [sem(f"tile_outputs_scattered{i}") for i in range(RX)]
        s_tx = sem("tile_transposed")
        s_xt = sem("tile_columns_ready")
        s_w1 = sem("first_weights_ready")
        s_up = sem("hidden_sums_ready")
        s_hid = sem("hidden_ready")
        s_dn = sem("output_sums_ready")
        s_yr = sem("tile_outputs_ready")
        s_w2r = sem("second_weights_ready")
        s_tpass = sem("gpsimd_tile_wait_passed")
        s_lpass = sem("sync_tile_wait_passed")
        s_apass = sem("scalar_output_wait_passed")

        def over_tiles(eng, step):
            for k in range(RX):
                step(0, k, k, True, True)
            with eng.Fori(1, NS // RX - 1) as i:
                for k in range(RX):
                    step(i, k, i * RX + k, True, True)
            for k in range(RX):
                i = NS // RX - 1
                step(i, k, i * RX + k, k < RX - 1, k < RX - 2)

        with nc.Block() as block:
            @block.sync
            def _(sp):
                def load(i, k, reused):
                    first = sp.value_load(tab[0:1, 1, bass.ds(i * RX + k, 1)], min_val=0,
                                          max_val=E * CAP + (NULL - 1) * P)
                    if reused:
                        sp.wait_ge(s_ys[k], i * 16)
                        sp.sem_inc(s_lpass, 1)
                    sp.dma_start(xr[k][:], xg_dram[bass.ds(first, P), :]).then_inc(s_xr[k], 16)

                for k in range(RX):
                    load(0, k, False)
                with sp.Fori(1, NS // RX) as i:
                    for k in range(RX):
                        load(i, k, True)

            @block.tensor
            def _(pe):
                pe.sem_inc(s_up, 2)
                pe.sem_inc(s_dn, 2)

                def turn(i, k, s):
                    pe.wait_ge(s_xr[k % RX], i * 16 + 16)
                    pe.wait_ge(s_xt, s + 1)
                    pe.transpose(ps[k % 2][:, 0:P], xr[k % RX][:, 0:D], ident[:]).then_inc(s_tx, 1)

                def up(k, s):
                    pe.wait_ge(s_xt, s + 3)
                    pe.wait_ge(s_w1, s + 1)
                    pe.wait_ge(s_hid, s + 1)
                    for f in range(FC):
                        cs = slice(f * P, (f + 1) * P)
                        mm = pe.matmul(ps[2 + k % 2][:, cs], w1b[k % 2][:, cs], xt[k % 2][:], start=True, stop=True)
                    mm.then_inc(s_up, 1)

                turn(0, 0, 0)
                turn(0, 1, 1)
                up(0, 0)

                def step(i, k, s, has_next, has_second):
                    if has_second:
                        turn(i + (k + 2) // RX, k + 2, s + 2)
                    if has_next:
                        up(k + 1, s + 1)
                    pe.wait_ge(s_hid, s + 3)
                    pe.wait_ge(s_w2r, s + 1)
                    pe.wait_ge(s_yr, s + 1)
                    for f in range(FC):
                        mm = pe.matmul(ps[4 + k % 2][:, 0:D], hid[k % 2][:, f, :], w2b[k % 2][:, f * D:(f + 1) * D],
                                       start=(f == 0), stop=(f == FC - 1))
                    mm.then_inc(s_dn, 1)

                over_tiles(pe, step)

            @block.scalar
            def _(act):
                act.sem_inc(s_hid, 2)

                def gelu(k, s):
                    act.wait_ge(s_up, s + 3)
                    act.wait_ge(s_dn, s + 1)
                    for f in range(FC):
                        op = act.activation(hid[k % 2][:, f, :], ps[2 + k % 2][:, f * P:(f + 1) * P], ACT.Gelu,
                                            bias=w1b[k % 2][:, FF + f:FF + f + 1])
                    op.then_inc(s_hid, 1)

                def weights(k, s):
                    e = act.value_load(tab[0:1, 0, bass.ds(s, 1)], min_val=0, max_val=E - 1)
                    act.wait_ge(s_hid, s + 1)
                    act.wait_ge(s_up, s + 1)
                    act.activation(w1b[k % 2][:].unsqueeze(1), w1a[:, bass.ds(e, 1), :], ACT.Copy).then_inc(s_w1, 1)

                act.preload_act_table_set("gelu_and_others")
                weights(0, 0)
                weights(1, 1)
                gelu(0, 0)

                def step(i, k, s, has_next, has_second):
                    if has_second:
                        weights(k, s + 2)
                    if has_next:
                        gelu(k + 1, s + 1)

                over_tiles(act, step)

            @block.gpsimd
            def _(pool):
                def step(i, k, s, has_next, has_second):
                    pool.wait_ge(s_yr, s + 3)
                    pool.sem_inc(s_tpass, 1)
                    pool.indirect_dma_start(yg_dram, bass.IndirectOffsetOnAxis(xr[k][:, D:].bitcast(U32), 0),
                                            yr[k][:], None).then_inc(s_ys[k], 16)

                over_tiles(pool, step)
                for k in range(RX):
                    pool.wait_ge(s_ys[k], 16 * (NS // RX))

            @block.vector
            def _(dve):
                dve.sem_inc(s_xt, 2)
                dve.sem_inc(s_yr, 2)

                def columns(k, s):
                    dve.wait_ge(s_tx, s + 1)
                    dve.wait_ge(s_up, s + 1)
                    dve.tensor_copy(xt[k % 2][:], ps[k % 2][:, 0:P]).then_inc(s_xt, 1)

                def weights(k, s):
                    e = dve.value_load(tab[0:1, 0, bass.ds(s, 1)], min_val=0, max_val=E - 1)
                    dve.wait_ge(s_dn, s + 1)
                    dve.wait_ge(s_yr, s + 1)
                    dve.tensor_scalar(w2b[k % 2][:].unsqueeze(1), w2all[:, bass.ds(e, 1), :], 1.0, None, ALU.mult)\
                        .then_inc(s_w2r, 1)

                columns(0, 0)
                columns(1, 1)
                weights(0, 0)

                def step(i, k, s, has_next, has_second):
                    if has_second:
                        columns(k, s + 2)
                    if has_next:
                        weights(k + 1, s + 1)
                    dve.wait_ge(s_dn, s + 3)
                    if not (isinstance(i, int) and i == 0):
                        dve.wait_ge(s_ys[k], i * 16)
                    dve.wait_ge(s_w2r, s + 1)
                    dve.tensor_tensor(yr[k][:], ps[4 + k % 2][:, 0:D], w2b[k % 2][:, FC * D:], ALU.add)\
                        .then_inc(s_yr, 1)

                over_tiles(dve, step)

        RY = 4
        yb = [sb(f"yb{i}", [P, 2, JT, D]) for i in range(RY)]
        s_yb = [sem(f"expert_outputs_loaded{i}") for i in range(RY)]
        s_o0 = sem("first_choice_added")
        s_o1 = sem("second_choice_added")
        s_out = [sem(f"output_written{i}") for i in range(2)]
        with nc.Block() as block:
            @block.sync
            def _(sp):
                yin = yg_dram[0:2 * N, :].rearrange("(x c j p) d -> c x p j d", x=2, j=JT, p=P)
                with sp.Fori(0, NCH // RY) as i:
                    for k in range(RY):
                        c = i * RY + k
                        sp.wait_ge(s_o1, c + 1)
                        sp.sem_inc(s_lpass, 1)
                        for x in range(2):
                            sp.dma_start(yb[k][:, x], yin[bass.ds(c, 1), x].rearrange("c p j d -> (c p) j d"))\
                              .then_inc(s_yb[k], 16)

            @block.vector
            def _(dve):
                dve.sem_inc(s_o1, RY)
                with dve.Fori(0, NCH // RY) as i:
                    for k in range(RY):
                        c = i * RY + k
                        dve.wait_ge(s_yb[k], i * 32 + 32)
                        for x in range(2):
                            for j in range(JT):
                                row = x1r[:, bass.ds(c * JT + j, 1), :]
                                op = dve.scalar_tensor_tensor(out=row, in0=yb[k][:, x, j, :].unsqueeze(1),
                                                              scalar=wts[:, x, bass.ds(c * JT + j, 1)], in1=row,
                                                              op0=ALU.mult, op1=ALU.add)
                            if x:
                                op.then_inc(s_o1, 1)
                            else:
                                op.then_inc(s_o0, 1)
                                dve.wait_ge(s_o0, c + 1)

            @block.scalar
            def _(act):
                with act.Fori(0, NCH // 2) as i:
                    for r in range(2):
                        c = i * 2 + r
                        act.wait_ge(s_o1, c + 1 + RY)
                        act.sem_inc(s_apass, 1)
                        act.dma_start(a["out"].rearrange("(c j p) d -> c p j d", j=JT, p=P)[bass.ds(c, 1)]
                                      .rearrange("c p j d -> (c p) j d"), x1r[:, bass.ds(c * JT, JT), :])\
                           .then_inc(s_out[r], 16)
                for r in range(2):
                    act.wait_ge(s_out[r], 16 * (NCH // 2))


def kernel(x, cond_1024, L0_cond_W, L0_cond_b, L0_cond_alpha, L0_attn_Wq, L0_attn_bq, L0_attn_Wk, L0_attn_bk,
           L0_attn_Wv, L0_attn_bv, L0_attn_Wo, L0_attn_bo, L0_attn_rel_k_emb, L0_attn_rel_v_emb,
           L0_cond2_Wx, L0_cond2_Wh, L0_cond2_b, L0_ffn_router_w, L0_ffn_expert_w1, L0_ffn_expert_b1,
           L0_ffn_expert_w2, L0_ffn_expert_b2):
    import numpy as np
    import concourse.bacc as bacc
    from concourse.bass_utils import run_bass_kernel_spmd

    f = np.asarray
    dh = np.arange(P).reshape(H, DH).T.ravel()
    arrays = {
        "xT": f(x).transpose(2, 1, 0),
        "condT": f(cond_1024).T,
        "wh": f(L0_cond_W)[:, :D].T, "wz": f(L0_cond_W)[:, D:].T,
        "wq": f(L0_attn_Wq)[dh].T, "wk": f(L0_attn_Wk)[dh].T, "wv": f(L0_attn_Wv).T, "wo": f(L0_attn_Wo).T,
        "wx2": f(L0_cond2_Wx), "wh2": f(L0_cond2_Wh),
        "cols": np.stack([f(v) for v in (L0_cond_b, L0_cond_alpha, f(L0_attn_bq)[dh], f(L0_attn_bk)[dh], L0_attn_bo,
                                         L0_cond2_b)], axis=1),
        "bv": f(L0_attn_bv),
        "relk": f(L0_attn_rel_k_emb)[REL:0:-1].T,
        "relv": f(L0_attn_rel_v_emb)[REL:0:-1],
        "ident": np.eye(P, dtype=np.float32),
        "w1T": f(L0_ffn_expert_w1).transpose(2, 0, 1),
        "w2T": f(L0_ffn_expert_w2).reshape(E, D, FC, P).transpose(3, 0, 2, 1),
        "b1c": f(L0_ffn_expert_b1).reshape(E, FC, P).transpose(2, 0, 1),
        "b2": f(L0_ffn_expert_b2),
        "rwT": f(L0_ffn_router_w).T,
        "iota": np.arange(E, dtype=np.float32),
        "upper": np.triu(np.ones((P, P), np.float32), 1),
        "ebase": np.arange(E, dtype=np.float32) * CAP,
        "mult": np.arange(MT, dtype=np.float32) * P,
        "tri": np.tril(np.ones((E, E), np.float32)).ravel(),
        "tiles": np.arange(NS, dtype=np.float32),
        "padid": (2 * N + np.arange(E + NULL)[None, :] * P + np.arange(P)[:, None]).astype(np.float32),
        "dest": (np.arange(2)[None, :, None] * N + np.arange(JT)[None, None, :] * P
                 + np.arange(P)[:, None, None]).reshape(P, 2 * JT).astype(np.float32),
    }
    arrays = {n: np.ascontiguousarray(v) for n, v in arrays.items()}
    nc = bacc.Bacc("TRN2", target_bir_lowering=False, num_devices=1)
    a = {n: nc.dram_tensor(f"in_{n}", v.shape, mybir.dt.from_np(v.dtype), kind="ExternalInput").ap()
         for n, v in arrays.items()}
    a["out"] = nc.dram_tensor("out_rows", (T * B, D), F32, kind="ExternalOutput").ap()
    build(nc, a)
    r = run_bass_kernel_spmd(nc, [{f"in_{n}": v for n, v in arrays.items()}], core_ids=[0])
    return r.results[0]["out_rows"].reshape(T, B, D).transpose(1, 0, 2)
```
